# Optimizing a Trainium2 kernel written in Bass

```python
import numpy as np
import jax
import jax.numpy as jnp

def _softmax(x, axis=-1):
    return jax.nn.softmax(x, axis=axis)

def _gelu(x):
    return jax.nn.gelu(x, approximate=True)

def _silu(x):
    return jax.nn.silu(x)

def _sigmoid(x):
    return jax.nn.sigmoid(x)

def _layernorm(x, axis=-1, eps=1e-05):
    m = jnp.mean(x, axis=axis, keepdims=True)
    v = jnp.var(x, axis=axis, keepdims=True)
    return (x - m) / jnp.sqrt(v + eps)

def _scatter_add(tgt, idx, src, axis=0):
    return tgt.at[idx].add(src)

def _segment_sum(src, seg, n):
    return jax.ops.segment_sum(src, seg, n)
kernel_name = 'mk_gnn_preln_d1_gnn_r8_87deab'

def setup_inputs(seed: int=0):
    np.random.seed(seed)
    _w = jnp.asarray

    def _rec_inputs():
        import jax
        import jax.numpy as jnp
        _gk = jax.random.key(seed)
        x = -8.776e-05 + 1 * jax.random.normal(jax.random.fold_in(_gk, 1), (2500, 256), jnp.float32)
        _s = jax.random.randint(jax.random.fold_in(_gk, 2), (40000,), 0, 2500, jnp.int32)
        _d = jax.random.randint(jax.random.fold_in(_gk, 3), (40000,), 0, 2500, jnp.int32)
        _loop = jnp.arange(2500, dtype=jnp.int32)
        src = jnp.concatenate([_s, _d, _loop])
        dst = jnp.concatenate([_d, _s, _loop])
        _o = jnp.argsort(dst, stable=True)
        src = src[_o]
        dst = dst[_o]
        edge_attr_256 = -8.513e-05 + 0.999844 * jax.random.normal(jax.random.fold_in(_gk, 12), (82500, 256), jnp.float32)
        return (x, src, dst, edge_attr_256)
    x, src, dst, edge_attr_256 = _rec_inputs()

    def _L0_gnn_setup():
        import jax, jax.numpy as jnp
        import numpy as np
        N_NODES = 2500
        N_EDGES = 40000
        IN_F = 256
        OUT_F = 256
        EDGE_F = 256

        def _mlp2(x, W1, b1, W2, b2):
            return jax.nn.relu(x @ W1 + b1) @ W2 + b2
        key = jax.random.key(seed)
        ks = jax.random.split(key, 12)

        def lin(k, fan_in, shape):
            bound = 1.0 / np.sqrt(fan_in)
            return jax.random.uniform(k, shape, jnp.float32, -bound, bound)
        node_feat = jax.random.normal(ks[0], (N_NODES, IN_F), jnp.float32)
        edge_feat = jax.random.normal(ks[1], (N_EDGES, EDGE_F), jnp.float32)
        src = jax.random.randint(ks[2], (N_EDGES,), 0, N_NODES, jnp.int32)
        dst = jax.random.randint(ks[3], (N_EDGES,), 0, N_NODES, jnp.int32)
        We1 = lin(ks[4], EDGE_F, (EDGE_F, 2 * EDGE_F))
        be1 = lin(ks[5], EDGE_F, (2 * EDGE_F,))
        We2 = lin(ks[6], 2 * EDGE_F, (2 * EDGE_F, IN_F))
        be2 = lin(ks[7], 2 * EDGE_F, (IN_F,))
        Wn1 = lin(ks[8], IN_F, (IN_F, 2 * IN_F))
        bn1 = lin(ks[9], IN_F, (2 * IN_F,))
        Wn2 = lin(ks[10], 2 * IN_F, (2 * IN_F, OUT_F))
        bn2 = lin(ks[11], 2 * IN_F, (OUT_F,))
        eps = jnp.zeros((1,), jnp.float32)
        return {'node_feat': node_feat, 'edge_feat': edge_feat, 'src': src, 'dst': dst, 'We1': We1, 'be1': be1, 'We2': We2, 'be2': be2, 'Wn1': Wn1, 'bn1': bn1, 'Wn2': Wn2, 'bn2': bn2, 'eps': eps}
    _L0_gnn_all = _L0_gnn_setup()
    _L0_gnn_in = {k: v for k, v in _L0_gnn_all.items() if k in ('We1', 'be1', 'We2', 'be2', 'Wn1', 'bn1', 'Wn2', 'bn2', 'eps')}
    del _L0_gnn_all
    return {'x': x, 'src': src, 'dst': dst, 'edge_attr_256': edge_attr_256, 'L0_gnn_We1': _L0_gnn_in['We1'], 'L0_gnn_be1': _L0_gnn_in['be1'], 'L0_gnn_We2': _L0_gnn_in['We2'], 'L0_gnn_be2': _L0_gnn_in['be2'], 'L0_gnn_Wn1': _L0_gnn_in['Wn1'], 'L0_gnn_bn1': _L0_gnn_in['bn1'], 'L0_gnn_Wn2': _L0_gnn_in['Wn2'], 'L0_gnn_bn2': _L0_gnn_in['bn2'], 'L0_gnn_eps': _L0_gnn_in['eps']}

def reference(x, src, dst, edge_attr_256, L0_gnn_We1, L0_gnn_be1, L0_gnn_We2, L0_gnn_be2, L0_gnn_Wn1, L0_gnn_bn1, L0_gnn_Wn2, L0_gnn_bn2, L0_gnn_eps):
    import jax
    import jax.numpy as jnp

    def _L0_gnn_ref(node_feat, edge_feat, src, dst, We1, be1, We2, be2, Wn1, bn1, Wn2, bn2, eps):
        import jax, jax.numpy as jnp
        import numpy as np
        N_NODES = 2500
        N_EDGES = 40000
        IN_F = 256
        OUT_F = 256
        EDGE_F = 256

        def _mlp2(x, W1, b1, W2, b2):
            return jax.nn.relu(x @ W1 + b1) @ W2 + b2
        e = _mlp2(edge_feat, We1, be1, We2, be2)
        msg = jax.nn.relu(node_feat[src] + e)
        out_h = jax.ops.segment_sum(msg, dst, num_segments=N_NODES)
        out = _mlp2((1.0 + eps[0]) * node_feat + out_h, Wn1, bn1, Wn2, bn2)
        return out
    h = jnp.maximum(_layernorm(x, axis=-1), 0.0)
    x = x + _L0_gnn_ref(h, edge_attr_256, src, dst, L0_gnn_We1, L0_gnn_be1, L0_gnn_We2, L0_gnn_be2, L0_gnn_Wn1, L0_gnn_bn1, L0_gnn_Wn2, L0_gnn_bn2, L0_gnn_eps)
    return x

_drawn_inputs = setup_inputs


def setup_inputs(seed=0):
    import zlib

    import numpy as np

    out = dict(_drawn_inputs(seed))
    spreads = {}
    factors = {'L0_gnn_be1': 3.998, 'L0_gnn_bn1': 8.0, 'L0_gnn_bn2': 8.0}
    for name, (base, spread) in spreads.items():
        noise = np.random.default_rng([zlib.crc32(name.encode()), seed]).standard_normal(out[name].shape)
        drawn = base * np.exp(spread * noise) if base else spread * noise
        out[name] = jnp.asarray(drawn.astype(out[name].dtype))
    for name, factor in factors.items():
        out[name] = (out[name] * factor).astype(out[name].dtype)
    return out
```

```python
from contextlib import ExitStack

import concourse.bass as bass
from concourse import mybir

ALU = mybir.AluOpType
ACT = mybir.ActivationFunctionType
AX = mybir.AxisListType
F32 = mybir.dt.float32
F32R = mybir.dt.float32r
I32 = mybir.dt.int32

P = 128
NODES = 2500
EDGES = 82500
F = 256
HID = 512
EB = 512
J = EB // P
KF = F // P
KH = HID // P
BLOCKS = -(-EDGES // EB)
OVERLAP = BLOCKS * EB - EDGES
WIN = -(-NODES // P)
TAILN = NODES - (WIN - 1) * P
GROUPS = WIN // J
LOOP = (BLOCKS - 4) // 2
LN_EPS = 1e-5
FAR = 8192.0


def gnn_program(nc, x, src, dst, edge, We1, be1, We2, be2, Wn1, bn1, Wn2, bn2, eps, out):
    assert WIN % J == 0 and BLOCKS % 2 == 0 and BLOCKS > P and EB == 4 * P
    ctx = ExitStack()
    with ctx:
        def sb(name, shape, dt=F32):
            return ctx.enter_context(nc.sbuf_tensor(name, shape, dt))

        def bank(name, shape):
            return ctx.enter_context(nc.psum_tensor(name, shape, F32))

        def sem(name):
            return ctx.enter_context(nc.semaphore(name))

        htab = nc.dram_tensor("h_rows", (WIN * P, F), F32, kind="Internal").ap()
        wtab = nc.dram_tensor("windows", (2 * P, 2), I32, kind="Internal").ap()

        h_sb = sb("h_sb", [P, WIN, F])
        acc = sb("acc", [P, WIN, F])
        w1 = {k: [sb(f"w1{k}_{p}", [P, KF, HID], F32R) for p in ("hi", "lo")] for k in ("e", "n")}
        w2 = {k: [sb(f"w2{k}_{p}", [P, KH, F], F32R) for p in ("hi", "lo")] for k in ("e", "n")}
        b1 = {k: sb(f"b1{k}", [P, KH]) for k in ("e", "n")}
        b2 = {k: sb(f"b2{k}", [P, F]) for k in ("e", "n")}
        ep1 = sb("ep1", [P, 1])
        e_in = [sb(f"e_in{i}", [P, J, F]) for i in range(2)]
        eT_hi = [sb(f"eT_hi{i}", [P, KF, EB], F32R) for i in range(2)]
        eT_lo = [sb(f"eT_lo{i}", [P, KF, EB], F32R) for i in range(2)]
        hid = sb("hid", [P, 2, EB])
        hid_hi = [sb(f"hid_hi{i}", [P, KH, EB], F32R) for i in range(2)]
        hid_lo = [sb(f"hid_lo{i}", [P, KH, EB], F32R) for i in range(2)]
        hg = [sb(f"hg{i}", [P, J, F]) for i in range(2)]
        pre = [sb(f"pre{q}", [P, 2, F]) for q in range(2)]
        msg_hi = [sb(f"msg_hi{i}", [P, J, F], F32R) for i in range(2)]
        msg_lo = [sb(f"msg_lo{i}", [P, J, F], F32R) for i in range(2)]
        sel = [sb(f"sel{i}", [P, J, P], F32R) for i in range(2)]
        sel_x = sb("sel_x", [P, J, P], F32R)
        node_id = sb("node_id", [P, WIN * P])
        part_id = sb("part_id", [P, 1])
        ident = sb("ident", [P, P])
        dst_i, src_i, dst_f, src_f, dst_far = (
            h_sb[:, 4 * n:4 * n + 4, :].rearrange("p t f -> p (t f)").rearrange("p (c e) -> p c e", c=2)
            for n in range(5))
        dst_i, src_i = dst_i.bitcast(I32), src_i.bitcast(I32)
        lim_f = sb("lim_f", [P, 2, 2])
        lim_i = sb("lim_i", [P, 2, 2], I32)
        win_i = sb("win_i", [P, 2, 2], I32)
        win_n = sb("win_n", [P, 2, 2], I32)
        win_row = sb("win_row", [1, 2 * BLOCKS], I32)
        dst_col = sb("dst_col", [P, BLOCKS, J])
        src_col = sb("src_col", [P, BLOCKS, J], I32)
        idx_now = [sb(f"idx_now{i}", [P, J], I32) for i in range(2)]
        stats = sb("stats", [P, WIN, 6])
        mv = sb("mv", [P, WIN, 2])
        var_e = sb("var_e", [P, WIN])
        std0 = sb("std0", [P, WIN])
        std1 = sb("std1", [P, WIN])
        std2 = sb("std2", [P, WIN])
        rstd = sb("rstd", [P, WIN])
        eps_t = sb("eps_t", [P, 1])
        mark = sb("mark", [1, 1])

        psT = [bank(f"psT{k}", [P, EB]) for k in range(KF)]
        psH = [bank(f"psH{i}", [P, EB]) for i in range(3)]
        psM = [bank(f"psM{q}", [P, 2, F]) for q in range(2)]
        psA = bank("psA", [P, EB])
        H_BANK = [0, 1, 2, 0]

        x_in = sem("x_in")
        idx_in = sem("idx_in")
        w_in = [sem(f"w_in{i}") for i in range(4)]
        small_in = sem("small_in")
        e_loaded = [sem(f"e_loaded{i}") for i in range(2)]
        gathered = [sem(f"gathered{i}") for i in range(2)]
        htab_out = sem("htab_out")
        wtab_out = sem("wtab_out")
        wrow_in = sem("wrow_in")
        out_done = [sem(f"out_done{i}") for i in range(2)]
        iota_done = sem("iota_done")
        prep = sem("prep")
        pads_done = sem("pads_done")
        ident_done = sem("ident_done")
        idx_float = sem("idx_float")
        idx_T = sem("idx_T")
        idx_cols = sem("idx_cols")
        win_done = sem("win_done")
        ln_var = sem("ln_var")
        ln_sqrt = sem("ln_sqrt")
        ln_z = sem("ln_z")
        acc_relu = sem("acc_relu")
        acc_init = sem("acc_init")
        h_done = sem("h_done")
        eps_done = sem("eps_done")
        whi_done = sem("whi_done")
        wlo_done = sem("wlo_done")
        t_done = sem("t_done")
        ehi_done = sem("ehi_done")
        elo_done = sem("elo_done")
        m1_done = sem("m1_done")
        hfull_done = sem("hfull_done")
        hlo_done = sem("hlo_done")
        m2_done = sem("m2_done")
        pre_done = sem("pre_done")
        mhi_done = sem("mhi_done")
        mlo_done = sem("mlo_done")
        sel_done = sem("sel_done")
        agg_done = sem("agg_done")
        added = sem("added")
        selx_done = sem("selx_done")
        aggx_done = sem("aggx_done")
        addedx = sem("addedx")
        idx_copied = sem("idx_copied")
        idx_ready = sem("idx_ready")
        x_back = [sem(f"x_back{i}") for i in range(2)]
        xb_done = sem("xb_done")

        block = ctx.enter_context(nc.Block())

        def staged(t, k):
            return t[:, :, :].rearrange("p j f -> p (j f)").rearrange("p (k h) -> p k h", k=k)

        def rows(t):
            return t.rearrange("(t p) f -> p t f", p=P)

        W1_IN, W2_IN, WN1_IN, WN2_IN = w_in
        FULLN = (WIN - 1) * P

        @block.sync
        def _(sp):
            sp.wait_ge(pads_done, 3)
            last = BLOCKS - 1 - P
            for tab, a in ((dst_i, dst), (src_i, src)):
                sp.dma_start(tab[:, 0, :], a[0:P * EB].rearrange("(s e) -> s e", e=EB)).then_inc(idx_in, 16)
                sp.dma_start(tab[0:last, 1, :],
                             a[P * EB:(BLOCKS - 1) * EB].rearrange("(s e) -> s e", e=EB)).then_inc(idx_in, 16)
            sp.dma_start(dst_i[last:last + 1, 1, OVERLAP:EB],
                         dst[(BLOCKS - 1) * EB:EDGES].rearrange("(o e) -> o e", o=1)).then_inc(idx_in, 16)
            sp.dma_start(src_i[last:last + 1, 1, :],
                         src[EDGES - EB:EDGES].rearrange("(o e) -> o e", o=1)).then_inc(idx_in, 16)

            def load(rnd, par, start):
                sp.dma_start(e_in[par][:, :, :],
                             edge[bass.ds(start, EB), :].rearrange("(p j) f -> p j f", j=J)
                             ).then_inc(e_loaded[par], 16)

            load(0, 0, 0)
            load(0, 1, EB)
            sp.dma_start(acc[0:TAILN, WIN - 1, :], x[FULLN:NODES, :]).then_inc(x_in, 16)
            sp.wait_ge(win_done, 1)
            sp.dma_start(wtab.rearrange("(c p) w -> p c w", p=P), win_n[:, :, :]).then_inc(wtab_out, 16)
            sp.wait_ge(wtab_out, 16)
            sp.dma_start(win_row[:, :], wtab[0:BLOCKS, :].rearrange("(o b) w -> o (b w)", o=1)).then_inc(wrow_in, 16)
            for g in range(GROUPS):
                sp.wait_ge(h_done, g + 1)
                sp.dma_start(rows(htab[g * EB:(g + 1) * EB, :]), h_sb[:, g * J:(g + 1) * J, :]
                             ).then_inc(htab_out, 16)

            with sp.Fori(0, (BLOCKS - 4) // 2) as i:
                for par in range(2):
                    sp.wait_ge(t_done, 4 * i + 2 * par + 2)
                    load(i + 1, par, (2 * i + par + 2) * EB)
            sp.wait_ge(t_done, 2 * (BLOCKS - 4) + 2)
            load(BLOCKS // 2 - 1, 0, (BLOCKS - 2) * EB)
            sp.wait_ge(t_done, 2 * (BLOCKS - 3) + 2)
            load(BLOCKS // 2 - 1, 1, EDGES - EB)

            def x_again(g):
                if g < 2:
                    sp.wait_ge(pre_done, 2 * (BLOCKS - 2 + g) + 2)
                if (g + 1) * J < WIN:
                    sp.dma_start(hg[g % 2][:, :, :], rows(x[g * EB:(g + 1) * EB, :])).then_inc(x_back[g % 2], 16)
                else:
                    sp.dma_start(hg[g % 2][:, 0:J - 1, :], rows(x[g * EB:FULLN, :])).then_inc(x_back[g % 2], 16)
                    sp.dma_start(hg[g % 2][0:TAILN, J - 1, :], x[FULLN:NODES, :]).then_inc(x_back[g % 2], 16)

            x_again(0)
            x_again(1)
            for g in range(GROUPS):
                for q in range(2):
                    t0 = g * J + 2 * q
                    sp.wait_ge(pre_done, 2 * (BLOCKS + g) + q + 1)
                    if t0 + 2 < WIN:
                        sp.dma_start(rows(out[t0 * P:(t0 + 2) * P, :]), pre[q][:, :, :]).then_inc(out_done[q], 16)
                    else:
                        sp.dma_start(out[t0 * P:(t0 + 1) * P, :], pre[q][:, 0, :]).then_inc(out_done[q], 16)
                        sp.dma_start(out[(t0 + 1) * P:NODES, :], pre[q][0:TAILN, 1, :]).then_inc(out_done[q], 16)
                if g + 2 < GROUPS:
                    x_again(g + 2)
            sp.wait_ge(out_done[0], 16 * GROUPS)
            sp.wait_ge(out_done[1], 16 * (GROUPS + 1))

        @block.gpsimd
        def _(pool):
            nc.gpsimd.iota(part_id[:, :], [[0, 1]], base=0, channel_multiplier=1,
                           allow_small_or_imprecise_dtypes=True).then_inc(iota_done, 1)
            nc.gpsimd.iota(node_id[:, :], [[1, WIN * P]], base=0, channel_multiplier=0,
                           allow_small_or_imprecise_dtypes=True).then_inc(iota_done, 1)

            def gather(b, rnd, par, wait=True):
                if wait:
                    pool.wait_ge(pre_done, 2 * b - 2)
                nc.gpsimd.tensor_copy(idx_now[par][:, :], src_col[:, bass.ds(b, 1), :].rearrange(
                    "p b j -> p (b j)")).then_inc(idx_copied, 1)
                copied = b + 1 if type(b) is int else pool.snap(b + 1)
                pool.wait_ge(idx_copied, copied)
                pool.sem_inc(idx_ready, 1)
                for j in range(J):
                    pool.indirect_dma_start(
                        out=hg[par][:, j, :], out_offset=None, in_=htab,
                        in_offset=bass.IndirectOffsetOnAxis(ap=idx_now[par][:, j:j + 1], axis=0),
                    ).then_inc(gathered[par], 16)

            pool.wait_ge(idx_cols, 4)
            pool.wait_ge(htab_out, 16 * GROUPS)
            gather(0, 0, 0, wait=False)
            gather(1, 0, 1, wait=False)
            with pool.Fori(0, (BLOCKS - 2) // 2) as i:
                for par in range(2):
                    gather(2 * i + 2 + par, i + 1, par)

        @block.tensor
        def _(pe):
            pe.wait_ge(ident_done, 1)
            idx_banks = [psM[0][:, :, :].rearrange("p a b -> p (a b)"),
                         psM[1][:, :, :].rearrange("p a b -> p (a b)"), psA[:, :], psH[2][:, :]]
            for n, (tab, c) in enumerate(((dst_f, 0), (dst_f, 1), (src_f, 0), (src_f, 1))):
                pe.wait_ge(idx_float, n // 2 + 1)
                for j in range(J):
                    last = nc.tensor.transpose(
                        idx_banks[n][:, j * P:(j + 1) * P],
                        tab[:, c, :].rearrange("s (p j) -> s j p", j=J)[:, j, :], ident[:, :])
                last.then_inc(idx_T, 1)

            def T(b, rnd, par, first=False, source=None):
                if source is None:
                    source = e_in[par]
                    pe.wait_ge(e_loaded[par], 16 * rnd + 16)
                for k in range(KF):
                    if not first:
                        pe.wait_ge(elo_done, 2 * b + k - 1)
                    for j in range(J):
                        last = nc.tensor.transpose(psT[k][:, j * P:(j + 1) * P],
                                                   source[:, j, k * P:(k + 1) * P], ident[:, :])
                    last.then_inc(t_done, 1)

            def M1(b, par, kind, first=False):
                hi, lo = w1[kind]
                pe.wait_ge(elo_done, 2 * b + 2)
                for m in range(KH):
                    if m == 3:
                        pe.wait_ge(hfull_done, 4 * b + 1)
                    elif not first:
                        pe.wait_ge(hfull_done, 4 * b if m == 0 else 4 * b - 3 + m)
                    ps = psH[H_BANK[m]][:, :]
                    c = slice(m * P, (m + 1) * P)
                    for k in range(KF):
                        nc.tensor.matmul(ps, hi[:, k, c], eT_hi[par][:, k, :], start=(k == 0), stop=False)
                        nc.tensor.matmul(ps, hi[:, k, c], eT_lo[par][:, k, :], start=False, stop=False)
                        last = nc.tensor.matmul(ps, lo[:, k, c], eT_hi[par][:, k, :],
                                                start=False, stop=(k == KF - 1))
                    last.then_inc(m1_done, 1)

            def M2(b, par, kind, first=False):
                hi, lo = w2[kind]
                pe.wait_ge(hlo_done, 4 * b + 4)
                for j in range(J):
                    if j % 2 == 0 and not first:
                        pe.wait_ge(pre_done, 2 * b - 1 + j // 2)
                    ps = psM[j // 2][:, j % 2, :]
                    c = slice(j * P, (j + 1) * P)
                    for k in range(KH):
                        nc.tensor.matmul(ps, hid_hi[par][:, k, c], hi[:, k, :], start=(k == 0), stop=False)
                        nc.tensor.matmul(ps, hid_hi[par][:, k, c], lo[:, k, :], start=False, stop=False)
                        last = nc.tensor.matmul(ps, hid_lo[par][:, k, c], hi[:, k, :],
                                                start=False, stop=(k == KH - 1))
                    last.then_inc(m2_done, 1)

            extra = pe.alloc_register("pe_further_windows")
            pe.reg_mov(extra, 0)

            def sum_window(par, s):
                for j in range(J):
                    nc.tensor.matmul(psA[:, 0:F], s[:, j, :], msg_hi[par][:, j, :], start=(j == 0), stop=False)
                    last = nc.tensor.matmul(psA[:, 0:F], s[:, j, :], msg_lo[par][:, j, :],
                                            start=False, stop=(j == J - 1))
                return last

            def AGG(b, par, first=False):
                more = pe.value_load(win_row[0:1, bass.ds(2 * b + 1, 1)], min_val=0, max_val=WIN - 1)
                before = pe.snap(extra, min_val=0, max_val=BLOCKS * WIN)
                pe.wait_ge(mlo_done, 2 * b + 2)
                pe.wait_ge(sel_done, b + 1)
                if not first:
                    pe.wait_ge(added, b)
                    pe.wait_ge(addedx, before + 1)
                sum_window(par, sel[par]).then_inc(agg_done, 1)
                with pe.If(more > 0):
                    with pe.Fori(1, more + 1) as w:
                        pe.wait_ge(added, b + 1)
                        pe.wait_ge(selx_done, before + w)
                        pe.wait_ge(addedx, before + w)
                        sum_window(par, sel_x).then_inc(aggx_done, 1)
                pe.reg_add(extra, extra, more)

            pe.wait_ge(idx_cols, 4)
            T(0, 0, 0, first=True)
            T(1, 0, 1)
            pe.wait_ge(wlo_done, 1)
            M1(0, 0, "e", first=True)
            T(2, 1, 0)
            M1(1, 1, "e")
            pe.wait_ge(wlo_done, 2)
            M2(0, 0, "e", first=True)
            pe.wait_ge(wrow_in, 16)
            T(3, 1, 1)
            M1(2, 0, "e")
            AGG(0, 0, first=True)
            M2(1, 1, "e")
            with pe.Fori(0, (BLOCKS - 4) // 2) as i:
                for u in range(2):
                    b = 2 * i + 3 + u
                    T(b + 1, i + 2, u)
                    M1(b, 1 - u, "e")
                    AGG(b - 2, 1 - u)
                    M2(b - 1, u, "e")
            b = BLOCKS - 1
            M1(b, 1, "e")
            AGG(b - 2, 1)
            M2(b - 1, 0, "e")
            AGG(b - 1, 0)
            M2(b, 1, "e")
            AGG(b, 1)
            n_all = pe.snap(extra, min_val=0, max_val=BLOCKS * WIN)
            pe.wait_ge(added, BLOCKS)
            pe.wait_ge(addedx, n_all + 1)
            pe.wait_ge(wlo_done, 4)
            for g in range(GROUPS + 1):
                b = BLOCKS + g
                if g == 0:
                    T(b, 0, 0, source=acc[:, 0:J, :])
                if g + 1 < GROUPS:
                    T(b + 1, 0, 0, source=acc[:, (g + 1) * J:(g + 2) * J, :])
                if g < GROUPS:
                    M1(b, b % 2, "n")
                if g > 0:
                    M2(b - 1, (b - 1) % 2, "n")

        @block.scalar
        def _(act):
            act.dma_start(staged(hg[0], KF),
                          We1.rearrange("(k p) h -> p k h", p=P)).then_inc(W1_IN, 16)
            act.dma_start(staged(hg[1], KH),
                          We2.rearrange("(k p) h -> p k h", p=P)).then_inc(W2_IN, 16)
            act.dma_start(acc[:, 0:WIN - 1, :], rows(x[0:FULLN, :])).then_inc(x_in, 16)
            with nc.allow_non_contiguous_dma(reason="512 biases, once"):
                act.dma_start(b1["e"][:, :], be1.rearrange("(m p) -> p m", p=P)).then_inc(small_in, 16)
                act.dma_start(b1["n"][:, :], bn1.rearrange("(m p) -> p m", p=P)).then_inc(small_in, 16)
            for k, b in (("e", be2), ("n", bn2)):
                act.dma_start(b2[k][:, :], b.rearrange("(o f) -> o f", o=1).to_broadcast([P, F])
                              ).then_inc(small_in, 16)
            act.dma_start(eps_t[:, :], eps.rearrange("(o f) -> o f", o=1).to_broadcast([P, 1])
                          ).then_inc(small_in, 16)

            def w_hi(w_sem, stage, k, dest):
                act.wait_ge(w_sem, 16)
                nc.scalar.copy(dest[:, :, :], staged(stage, k)).then_inc(whi_done, 1)

            def E_HI(b, par, first=False):
                for k in range(KF):
                    act.wait_ge(t_done, 2 * b + k + 1)
                    if not first:
                        act.wait_ge(m1_done, 4 * b - 4)
                    nc.scalar.copy(eT_hi[par][:, k, :], psT[k][:, :]).then_inc(ehi_done, 1)

            def HIDDEN(b, par, kind, first=0):
                if not first:
                    act.wait_ge(m2_done, 4 * b - 4)
                for m in range(KH):
                    act.wait_ge(m1_done, 4 * b + m + 1)
                    nc.scalar.activation(hid_hi[par][:, m, :], psH[H_BANK[m]][:, :], ACT.Relu,
                                         bias=b1[kind][:, m:m + 1])
                    if first < 2 or m >= 2:
                        act.wait_ge(hlo_done, 4 * b + m - 1)
                    nc.scalar.activation(hid[:, m % 2, :], psH[H_BANK[m]][:, :], ACT.Relu,
                                         bias=b1[kind][:, m:m + 1]).then_inc(hfull_done, 1)

            def MSG_HI(b, par):
                for q in range(2):
                    act.wait_ge(pre_done, 2 * b + q + 1)
                    nc.scalar.activation(msg_hi[par][:, 2 * q:2 * q + 2, :], pre[q][:, :, :], ACT.Relu
                                         ).then_inc(mhi_done, 1)

            w_hi(W1_IN, hg[0], KF, w1["e"][0])
            w_hi(W2_IN, hg[1], KH, w2["e"][0])
            act.wait_ge(ln_var, 1)
            nc.scalar.activation(std0[:, :], var_e[:, :], ACT.Sqrt).then_inc(ln_sqrt, 1)
            E_HI(0, 0, first=True)
            E_HI(1, 1, first=True)
            for g in range(GROUPS):
                act.wait_ge(ln_z, g + 1)
                nc.scalar.activation(acc[:, g * J:(g + 1) * J, :], h_sb[:, g * J:(g + 1) * J, :], ACT.Relu
                                     ).then_inc(acc_relu, 1)
            act.wait_ge(small_in, 80)
            HIDDEN(0, 0, "e", first=2)
            act.wait_ge(eps_done, 1)
            for g in range(GROUPS):
                act.wait_ge(acc_relu, g + 1)
                nc.scalar.activation(acc[:, g * J:(g + 1) * J, :], acc[:, g * J:(g + 1) * J, :], ACT.Copy,
                                     scale=ep1[:, 0:1]).then_inc(acc_init, 1)
            E_HI(2, 0)
            HIDDEN(1, 1, "e", first=1)
            MSG_HI(0, 0)
            with act.Fori(0, LOOP) as i:
                for u in range(2):
                    b = 2 * i + 2 + u
                    E_HI(b + 1, 1 - u)
                    HIDDEN(b, u, "e")
                    MSG_HI(b - 1, 1 - u)
            b = BLOCKS - 2
            E_HI(b + 1, 1)
            HIDDEN(b, 0, "e")
            MSG_HI(b - 1, 1)
            act.wait_ge(t_done, 2 * BLOCKS)
            act.dma_start(staged(e_in[0], KF),
                          Wn1.rearrange("(k p) h -> p k h", p=P)).then_inc(WN1_IN, 16)
            act.dma_start(staged(e_in[1], KH),
                          Wn2.rearrange("(k p) h -> p k h", p=P)).then_inc(WN2_IN, 16)
            HIDDEN(b + 1, 1, "e")
            MSG_HI(b, 0)
            w_hi(WN1_IN, e_in[0], KF, w1["n"][0])
            w_hi(WN2_IN, e_in[1], KH, w2["n"][0])
            MSG_HI(b + 1, 1)
            for g in range(GROUPS):
                b = BLOCKS + g
                if g == 0:
                    E_HI(b, b % 2)
                if g + 1 < GROUPS:
                    E_HI(b + 1, (b + 1) % 2)
                HIDDEN(b, b % 2, "n")

        @block.vector
        def _(dve):
            step = [0]

            def chain(ins):
                step[0] += 1
                ins.then_inc(prep, 1)
                dve.wait_ge(prep, step[0])

            nc.vector.memset(src_i[:, 1, :], 0).then_inc(pads_done, 1)
            nc.vector.memset(dst_i[:, 1, :], -1).then_inc(pads_done, 1)
            nc.vector.memset(acc[:, WIN - 1, :], 0.0).then_inc(pads_done, 1)
            dve.wait_ge(iota_done, 2)
            nc.vector.tensor_scalar(ident[:, :], node_id[:, 0:P], part_id[:, 0:1], None, ALU.is_equal
                                    ).then_inc(ident_done, 1)
            dve.wait_ge(idx_in, 16 * 6)
            nc.vector.tensor_copy(dst_f[:, :, :], dst_i[:, :, :]).then_inc(idx_float, 1)
            nc.vector.tensor_copy(src_f[:, :, :], src_i[:, :, :]).then_inc(idx_float, 1)
            def w_lo(n, stage, k, hi, lo):
                dve.wait_ge(whi_done, n + 1)
                nc.vector.tensor_tensor(lo[:, :, :], staged(stage, k), hi[:, :, :].bitcast(F32), ALU.subtract
                                        ).then_inc(wlo_done, 1)

            w_lo(0, hg[0], KF, *w1["e"])

            dve.wait_ge(idx_float, 1)
            chain(nc.vector.tensor_scalar(dst_far[:, :, :], dst_f[:, :, :], 0.0, FAR, ALU.is_lt, ALU.mult))
            chain(nc.vector.tensor_tensor(dst_far[:, :, :], dst_far[:, :, :], dst_f[:, :, :], ALU.add))
            nc.vector.tensor_reduce(lim_f[:, :, 0:1], dst_far[:, :, :], AX.X, ALU.min)
            chain(nc.vector.tensor_reduce(lim_f[:, :, 1:2], dst_f[:, :, :], AX.X, ALU.max))
            chain(nc.vector.tensor_copy(lim_i[:, :, :], lim_f[:, :, :]))
            chain(nc.vector.tensor_scalar(win_i[:, :, :], lim_i[:, :, :], 7, None, ALU.arith_shift_right))
            nc.vector.tensor_copy(win_n[:, :, 0:1], win_i[:, :, 0:1])
            chain(nc.vector.tensor_tensor(win_n[:, :, 1:2], win_i[:, :, 1:2], win_i[:, :, 0:1], ALU.subtract))
            nc.vector.memset(mark[:, :], 0.0).then_inc(win_done, 1)
            idx_ps = [psM[0][:, :, :].rearrange("p a b -> p (a b)"),
                      psM[1][:, :, :].rearrange("p a b -> p (a b)"), psA[:, :], psH[2][:, :]]
            for n, (col, c) in enumerate(((dst_col, 0), (dst_col, 1), (src_col, 0), (src_col, 1))):
                dve.wait_ge(idx_T, n + 1)
                many = min(P, BLOCKS - c * P)
                nc.vector.tensor_copy(col[:, c * P:c * P + many, :],
                                      idx_ps[n].rearrange("p (j s) -> p s j", j=J)[:, 0:many, :]
                                      ).then_inc(idx_cols, 1)

            dve.wait_ge(x_in, 32)
            for t in range(WIN):
                last = nc.vector.bn_stats(stats[:, t, :], acc[:, t, :])
            chain(last)
            for t in range(WIN):
                last = nc.vector.bn_aggr(mv[:, t, :], stats[:, t, :])
            chain(last)
            nc.vector.tensor_scalar(var_e[:, :], mv[:, :, 1], LN_EPS, None, ALU.add).then_inc(ln_var, 1)
            w_lo(1, hg[1], KH, *w2["e"])
            dve.wait_ge(small_in, 80)
            nc.vector.tensor_scalar(ep1[:, :], eps_t[:, :], 1.0, None, ALU.add).then_inc(eps_done, 1)
            dve.wait_ge(ln_sqrt, 1)
            chain(nc.vector.reciprocal(std1[:, :], std0[:, :]))
            chain(nc.vector.tensor_tensor(std1[:, :], std1[:, :], var_e[:, :], ALU.mult))
            chain(nc.vector.tensor_tensor(std1[:, :], std1[:, :], std0[:, :], ALU.add))
            chain(nc.vector.tensor_scalar(std2[:, :], std1[:, :], 0.5, None, ALU.mult))
            chain(nc.vector.reciprocal(rstd[:, :], std2[:, :]))
            for g in range(GROUPS):
                for t in range(g * J, (g + 1) * J):
                    last = nc.vector.tensor_scalar(h_sb[:, t, :], acc[:, t, :], mv[:, t, 0:1], rstd[:, t:t + 1],
                                                   ALU.subtract, ALU.mult)
                last.then_inc(ln_z, 1)

            def E_LO(b, par, first=False):
                for k in range(KF):
                    dve.wait_ge(ehi_done, 2 * b + k + 1)
                    if k == 0 and not first:
                        dve.wait_ge(m1_done, 4 * b - 4)
                    nc.vector.tensor_tensor(eT_lo[par][:, k, :], psT[k][:, :], eT_hi[par][:, k, :].bitcast(F32),
                                            ALU.subtract).then_inc(elo_done, 1)

            def HID_LO(b, par, first=False):
                for m in range(KH):
                    dve.wait_ge(hfull_done, 4 * b + m + 1)
                    if m == 0 and not first:
                        dve.wait_ge(m2_done, 4 * b - 4)
                    nc.vector.tensor_tensor(hid_lo[par][:, m, :], hid[:, m % 2, :],
                                            hid_hi[par][:, m, :].bitcast(F32), ALU.subtract).then_inc(hlo_done, 1)

            def MSG(b, rnd, par):
                for q in range(2):
                    dve.wait_ge(m2_done, 4 * b + 2 * q + 2)
                    if q == 0:
                        dve.wait_ge(gathered[par], 16 * J * rnd + 16 * J)
                    nc.vector.tensor_tensor(pre[q][:, :, :], psM[q][:, :, :], hg[par][:, 2 * q:2 * q + 2, :],
                                            ALU.add).then_inc(pre_done, 1)
                for q in range(2):
                    dve.wait_ge(mhi_done, 2 * b + q + 1)
                    nc.vector.scalar_tensor_tensor(msg_lo[par][:, 2 * q:2 * q + 2, :], pre[q][:, :, :], 0.0,
                                                   msg_hi[par][:, 2 * q:2 * q + 2, :].bitcast(F32),
                                                   ALU.max, ALU.subtract).then_inc(mlo_done, 1)

            extra = dve.alloc_register("dve_further_windows")
            dve.reg_mov(extra, 0)

            def select(dest, b, w):
                return nc.vector.tensor_tensor(
                    dest[:, :, :],
                    node_id[:, bass.ds(w * P, P)].rearrange("p (o c) -> p o c", o=1).to_broadcast([P, J, P]),
                    dst_col[:, bass.ds(b, 1), :].rearrange("p o j -> p j o").to_broadcast([P, J, P]),
                    ALU.is_equal)

            def add_window(w):
                a = acc[:, bass.ds(w, 1), :].rearrange("p o f -> p (o f)")
                return nc.vector.tensor_tensor(a, psA[:, 0:F], a, ALU.add)

            def windows(b):
                w_lo = dve.value_load(win_row[0:1, bass.ds(2 * b, 1)], min_val=0, max_val=WIN - 1)
                more = dve.value_load(win_row[0:1, bass.ds(2 * b + 1, 1)], min_val=0, max_val=WIN - 1)
                return w_lo, more

            further = dve.alloc_register("dve_further_window")

            def window_at(w_lo, k):
                dve.reg_add(further, w_lo, k)
                return dve.snap(further, min_val=0, max_val=WIN - 1)

            def SEL(b, par, w, first=False):
                w_lo, more = w
                if not first:
                    dve.wait_ge(agg_done, b - 1)
                select(sel[par], b, w_lo).then_inc(sel_done, 1)
                with dve.If(more > 0):
                    select(sel_x, b, window_at(w_lo, 1)).then_inc(selx_done, 1)

            def ADD(b, w):
                w_lo, more = w
                dve.wait_ge(agg_done, b + 1)
                add_window(w_lo).then_inc(added, 1)
                with dve.If(more > 0):
                    before = dve.snap(extra, min_val=0, max_val=BLOCKS * WIN)
                    with dve.Fori(1, more + 1) as k:
                        dve.wait_ge(aggx_done, before + k)
                        add_window(window_at(w_lo, k)).then_inc(addedx, 1)
                        with dve.If(more > k):
                            select(sel_x, b, window_at(w_lo, k + 1)
                                   ).then_inc(selx_done, 1)
                dve.reg_add(extra, extra, more)

            E_LO(0, 0, first=True)
            E_LO(1, 1, first=True)
            for g in range(GROUPS):
                dve.wait_ge(acc_relu, g + 1)
                h = h_sb[:, g * J:(g + 1) * J, :]
                nc.vector.scalar_tensor_tensor(
                    h, h, 0.0, b2["e"][:, :].rearrange("p (o f) -> p o f", o=1).to_broadcast([P, J, F]),
                    ALU.max, ALU.add).then_inc(h_done, 1)
            HID_LO(0, 0, first=True)
            E_LO(2, 0)
            HID_LO(1, 1, first=True)
            MSG(0, 0, 0)
            nc.vector.memset(mark[:, :], 0.0).then_inc(addedx, 1)
            dve.wait_ge(wrow_in, 16)
            dve.wait_ge(acc_init, GROUPS)
            for b in (2, 3):
                E_LO(b + 1, (b + 1) % 2)
                w = windows(b - 2)
                SEL(b - 2, b % 2, w, first=True)
                HID_LO(b, b % 2)
                ADD(b - 2, w)
                MSG(b - 1, (b - 1) // 2, (b - 1) % 2)
            with dve.Fori(0, LOOP - 1) as i:
                for u in range(2):
                    b = 2 * i + 4 + u
                    E_LO(b + 1, 1 - u)
                    w = windows(b - 2)
                    SEL(b - 2, u, w)
                    HID_LO(b, u)
                    ADD(b - 2, w)
                    MSG(b - 1, i + 1 + u, 1 - u)
            for b in range(BLOCKS - 2, BLOCKS + 2):
                if b + 1 < BLOCKS:
                    E_LO(b + 1, (b + 1) % 2)
                w = windows(b - 2)
                SEL(b - 2, b % 2, w)
                if b < BLOCKS:
                    HID_LO(b, b % 2)
                ADD(b - 2, w)
                if b - 1 < BLOCKS:
                    MSG(b - 1, (b - 1) // 2, (b - 1) % 2)
                if b == BLOCKS:
                    w_lo(2, e_in[0], KF, *w1["n"])
                    w_lo(3, e_in[1], KH, *w2["n"])
            for g in range(GROUPS + 1):
                b = BLOCKS + g
                if g == 0:
                    E_LO(b, b % 2)
                if g + 1 < GROUPS:
                    E_LO(b + 1, (b + 1) % 2)
                if g < GROUPS:
                    dve.wait_ge(x_back[g % 2], 16 * (g // 2 + 1 + (g == GROUPS - 1)))
                    xb = hg[g % 2][:, :, :]
                    nc.vector.tensor_tensor(
                        xb, xb, b2["n"][:, :].rearrange("p (o f) -> p o f", o=1).to_broadcast([P, J, F]),
                        ALU.add).then_inc(xb_done, 1)
                    HID_LO(b, b % 2)
                if g > 0:
                    dve.wait_ge(xb_done, g)
                    for q in range(2):
                        dve.wait_ge(m2_done, 4 * (b - 1) + 2 * q + 2)
                        if g > 1:
                            dve.wait_ge(out_done[q], 16 * (g - 1))
                        nc.vector.tensor_tensor(pre[q][:, :, :], psM[q][:, :, :], hg[(g - 1) % 2][:, 2 * q:2 * q + 2, :],
                                                ALU.add).then_inc(pre_done, 1)


_INS = ["x", "src", "dst", "edge_attr_256", "L0_gnn_We1", "L0_gnn_be1", "L0_gnn_We2", "L0_gnn_be2",
        "L0_gnn_Wn1", "L0_gnn_bn1", "L0_gnn_Wn2", "L0_gnn_bn2", "L0_gnn_eps"]


def kernel(**inputs):
    import numpy as _np
    import concourse.bacc as _bacc
    from concourse import mybir as _mybir
    from concourse.bass_utils import run_bass_kernel_spmd as _run

    nc = _bacc.Bacc("TRN2", target_bir_lowering=False, num_devices=1)
    arrays, args = {}, []
    for name in _INS:
        a = _np.ascontiguousarray(inputs[name])
        arrays[f"in_{name}_dram"] = a
        args.append(nc.dram_tensor(f"in_{name}_dram", a.shape, _mybir.dt.from_np(a.dtype), kind="ExternalInput").ap())
    args.append(nc.dram_tensor("out_0_dram", (NODES, F), _mybir.dt.float32, kind="ExternalOutput").ap())
    gnn_program(nc, *args)
    r = _run(nc, [arrays], core_ids=[0])
    return r.results[0]["out_0_dram"]
```

```python
from contextlib import ExitStack

import concourse.bass as bass
from concourse import mybir

ALU = mybir.AluOpType
ACT = mybir.ActivationFunctionType
AX = mybir.AxisListType
F32 = mybir.dt.float32
F32R = mybir.dt.float32r
I32 = mybir.dt.int32

P = 128
NODES = 2500
EDGES = 82500
F = 256
HID = 512
EB = 512
J = EB // P
Q = 32
S = EB // Q
KF = F // P
KH = HID // P
BLOCKS = -(-EDGES // EB)
OVERLAP = BLOCKS * EB - EDGES
WIN = -(-NODES // P)
TAILN = NODES - (WIN - 1) * P
GROUPS = WIN // J
POOL_GROUPS = 3
LOOP = (BLOCKS - 4) // 2
LN_EPS = 1e-5
FAR = 8192


def gnn_program(nc, x, src, dst, edge, We1, be1, We2, be2, Wn1, bn1, Wn2, bn2, eps, out):
    assert WIN % J == 0 and BLOCKS % 2 == 0 and BLOCKS > P and EB == 4 * P
    ctx = ExitStack()
    with ctx:
        def sb(name, shape, dt=F32):
            return ctx.enter_context(nc.sbuf_tensor(name, shape, dt))

        def bank(name, shape):
            return ctx.enter_context(nc.psum_tensor(name, shape, F32))

        def sem(name):
            return ctx.enter_context(nc.semaphore(name))

        htab = nc.dram_tensor("h_rows", (WIN * P, F), F32, kind="Internal").ap()
        wtab = nc.dram_tensor("windows", (2 * P, 4), I32, kind="Internal").ap()
        ltab = nc.dram_tensor("smallest", (2 * P,), I32, kind="Internal").ap()

        h_sb = sb("h_sb", [P, WIN, F])
        acc = sb("acc", [P, WIN, F])
        w1 = {k: [sb(f"w1{k}_{p}", [P, KF, HID], F32R) for p in ("hi", "lo")] for k in ("e", "n")}
        w2 = {k: [sb(f"w2{k}_{p}", [P, KH, F], F32R) for p in ("hi", "lo")] for k in ("e", "n")}
        b1 = {k: sb(f"b1{k}", [P, KH]) for k in ("e", "n")}
        b2 = {k: sb(f"b2{k}", [P, F]) for k in ("e", "n")}
        ep1 = sb("ep1", [P, 1])
        e_in = [sb(f"e_in{i}", [P, S, 2 * Q]) for i in range(2)]
        eT = sb("eT", [P, KF, EB])
        eT_hi = [sb(f"eT_hi{i}", [P, KF, EB], F32R) for i in range(2)]
        eT_lo = [sb(f"eT_lo{i}", [P, KF, EB], F32R) for i in range(2)]
        hid = sb("hid", [P, 2, EB])
        hid_hi = [sb(f"hid_hi{i}", [P, KH, EB], F32R) for i in range(2)]
        hid_lo = [sb(f"hid_lo{i}", [P, KH, EB], F32R) for i in range(2)]
        hg = [sb(f"hg{i}", [P, J, F]) for i in range(2)]
        pre = [sb(f"pre{q}", [P, 2, F]) for q in range(2)]
        msg_hi = [sb(f"msg_hi{i}", [P, J, F], F32R) for i in range(2)]
        msg_lo = [sb(f"msg_lo{i}", [P, J, F], F32R) for i in range(2)]
        sel = [sb(f"sel{i}", [P, J, P], F32R) for i in range(2)]
        sel_x = sb("sel_x", [P, J, P], F32R)
        node_id = sb("node_id", [P, WIN * P])
        part_id = sb("part_id", [P, 1])
        ident = sb("ident", [P, P])
        dst_i = sb("dst_i", [P, 2, EB], I32)
        dst_f = sb("dst_f", [P, 2, EB])
        src_i, src_f = (
            h_sb[:, 4 * n:4 * n + 4, :].rearrange("p t f -> p (t f)").rearrange("p (c e) -> p c e", c=2)
            for n in range(2))
        src_i = src_i.bitcast(I32)
        lim_f = sb("lim_f", [P, 2, 2])
        lim_i = sb("lim_i", [P, 2, 2], I32)
        win_i = sb("win_i", [P, 2, 2], I32)
        wide = sb("wide", [P, 2, 2])
        win_t = sb("win_t", [P, 2, 4], I32)
        lo_mod = sb("lo_mod", [P, 2], I32)
        win_row = sb("win_row", [1, 4 * BLOCKS], I32)
        lo_row = sb("lo_row", [P, BLOCKS], I32)
        in_first = sb("in_first", [P, BLOCKS])
        in_next = sb("in_next", [P, BLOCKS])
        dst_col = sb("dst_col", [P, BLOCKS, J])
        mod_col = sb("mod_col", [P, BLOCKS, J])
        src_col = sb("src_col", [P, BLOCKS, J], I32)
        idx_now = [sb(f"idx_now{i}", [P, J], I32) for i in range(2)]
        stats = sb("stats", [P, WIN, 6])
        mv = sb("mv", [P, WIN, 2])
        var_e = sb("var_e", [P, WIN])
        std0 = sb("std0", [P, WIN])
        std1 = sb("std1", [P, WIN])
        std2 = sb("std2", [P, WIN])
        rstd = sb("rstd", [P, WIN])
        eps_t = sb("eps_t", [P, 1])
        mark = sb("mark", [1, 1])

        psT = [bank(f"psT{k}", [P, EB]) for k in range(KF)]
        psH = [bank(f"psH{i}", [P, EB]) for i in range(3)]
        psM = [bank(f"psM{q}", [P, 2, F]) for q in range(2)]
        psA = bank("psA", [P, EB])
        H_BANK = [0, 1, 2, 0]

        x_in = [sem(f"x_in{g}") for g in range(GROUPS)]
        src_in = sem("src_in")
        dst_in = sem("dst_in")
        w_in = [sem(f"w_in{i}") for i in range(4)]
        small_in = sem("small_in")
        e_loaded = [sem(f"e_loaded{i}") for i in range(2)]
        gathered = [sem(f"gathered{i}") for i in range(2)]
        htab_out = sem("htab_out")
        wtab_out = sem("wtab_out")
        wrow_in = sem("wrow_in")
        out_done = [sem(f"out_done{i}") for i in range(2)]
        iota_done = sem("iota_done")
        iota_wide = sem("iota_wide")
        prep = sem("prep")
        pads_done = sem("pads_done")
        ident_done = sem("ident_done")
        src_float = sem("src_float")
        dst_float = sem("dst_float")
        src_T = sem("src_T")
        dst_T = sem("dst_T")
        src_cols = sem("src_cols")
        dst_cols = sem("dst_cols")
        win_done = sem("win_done")
        ln_var = sem("ln_var")
        ln_sqrt = sem("ln_sqrt")
        ln_z = sem("ln_z")
        acc_relu = sem("acc_relu")
        acc_init = sem("acc_init")
        h_pool = sem("h_pool")
        h_dve = sem("h_dve")
        eps_done = sem("eps_done")
        whi_done = sem("whi_done")
        wlo_done = sem("wlo_done")
        tr_done = sem("tr_done")
        ehi_done = sem("ehi_done")
        elo_done = sem("elo_done")
        t_done = sem("t_done")
        nhi_done = sem("nhi_done")
        nlo_done = sem("nlo_done")
        m1_done = sem("m1_done")
        hfull_done = sem("hfull_done")
        hlo_done = sem("hlo_done")
        m2_done = sem("m2_done")
        pre_done = sem("pre_done")
        mhi_done = sem("mhi_done")
        mlo_done = sem("mlo_done")
        sel_done = sem("sel_done")
        agg_done = sem("agg_done")
        added = sem("added")
        selx_done = sem("selx_done")
        aggx_done = sem("aggx_done")
        addedx = sem("addedx")
        idx_copied = sem("idx_copied")
        idx_ready = sem("idx_ready")
        x_back = [sem(f"x_back{i}") for i in range(2)]
        xb_done = sem("xb_done")

        block = ctx.enter_context(nc.Block())

        def staged(t, k):
            return t[:, :, :].rearrange("p a b -> p (a b)").rearrange("p (k h) -> p k h", k=k)

        def rows(t):
            return t.rearrange("(t p) f -> p t f", p=P)

        W1_IN, W2_IN, WN1_IN, WN2_IN = w_in
        FULLN = (WIN - 1) * P

        @block.sync
        def _(sp):
            sp.wait_ge(pads_done, 3)
            last = BLOCKS - 1 - P
            sp.dma_start(src_i[:, 0, :], src[0:P * EB].rearrange("(s e) -> s e", e=EB)).then_inc(src_in, 16)
            sp.dma_start(src_i[0:last, 1, :],
                         src[P * EB:(BLOCKS - 1) * EB].rearrange("(s e) -> s e", e=EB)).then_inc(src_in, 16)
            sp.dma_start(src_i[last:last + 1, 1, :],
                         src[EDGES - EB:EDGES].rearrange("(o e) -> o e", o=1)).then_inc(src_in, 16)
            def load(par, start):
                for q in range(P // Q):
                    sp.dma_start(e_in[par][q * Q:(q + 1) * Q, :, :],
                                 edge[bass.ds(start, EB), 2 * Q * q:2 * Q * (q + 1)].rearrange(
                                     "(s g) f -> s g f", g=S)).then_inc(e_loaded[par], 16)

            load(0, 0)
            for g in range(GROUPS):
                full = min((g + 1) * EB, FULLN)
                sp.dma_start(acc[:, g * J:full // P, :], rows(x[g * EB:full, :])).then_inc(x_in[g], 16)
            sp.dma_start(acc[0:TAILN, WIN - 1, :], x[FULLN:NODES, :]).then_inc(x_in[GROUPS - 1], 16)
            load(1, EB)
            sp.dma_start(dst_i[:, 0, :], dst[0:P * EB].rearrange("(s e) -> s e", e=EB)).then_inc(dst_in, 16)
            sp.dma_start(dst_i[0:last, 1, :],
                         dst[P * EB:(BLOCKS - 1) * EB].rearrange("(s e) -> s e", e=EB)).then_inc(dst_in, 16)
            sp.dma_start(dst_i[last:last + 1, 1, OVERLAP:EB],
                         dst[(BLOCKS - 1) * EB:EDGES].rearrange("(o e) -> o e", o=1)).then_inc(dst_in, 16)
            for g in range(GROUPS):
                if g < POOL_GROUPS:
                    sp.wait_ge(h_pool, g + 1)
                else:
                    sp.wait_ge(h_dve, g - POOL_GROUPS + 1)
                sp.dma_start(rows(htab[g * EB:(g + 1) * EB, :]), h_sb[:, g * J:(g + 1) * J, :]
                             ).then_inc(htab_out, 16)
            sp.wait_ge(win_done, 4)
            sp.dma_start(wtab.rearrange("(c p) w -> p c w", p=P), win_t[:, :, :]).then_inc(wtab_out, 16)
            with nc.allow_non_contiguous_dma(reason="256 numbers, once"):
                sp.dma_start(ltab.rearrange("(c p) -> p c", p=P), lo_mod[:, :]).then_inc(wtab_out, 16)
            sp.wait_ge(wtab_out, 32)
            sp.dma_start(win_row[:, :], wtab[0:BLOCKS, :].rearrange("(o b) w -> o (b w)", o=1)
                         ).then_inc(wrow_in, 16)
            sp.dma_start(lo_row[:, :], ltab[0:BLOCKS].rearrange("(o b) -> o b", o=1).to_broadcast([P, BLOCKS])
                         ).then_inc(wrow_in, 16)

            with sp.Fori(0, (BLOCKS - 4) // 2) as i:
                for par in range(2):
                    sp.wait_ge(tr_done, 2 * i + par + 1)
                    load(par, (2 * i + par + 2) * EB)
            sp.wait_ge(tr_done, BLOCKS - 3)
            load(0, (BLOCKS - 2) * EB)
            sp.wait_ge(tr_done, BLOCKS - 2)
            load(1, EDGES - EB)

            def x_again(g):
                if g < 2:
                    sp.wait_ge(pre_done, 2 * (BLOCKS - 2 + g) + 2)
                if (g + 1) * J < WIN:
                    sp.dma_start(hg[g % 2][:, :, :], rows(x[g * EB:(g + 1) * EB, :])).then_inc(x_back[g % 2], 16)
                else:
                    sp.dma_start(hg[g % 2][:, 0:J - 1, :], rows(x[g * EB:FULLN, :])).then_inc(x_back[g % 2], 16)
                    sp.dma_start(hg[g % 2][0:TAILN, J - 1, :], x[FULLN:NODES, :]).then_inc(x_back[g % 2], 16)

            x_again(0)
            x_again(1)
            for g in range(GROUPS):
                for q in range(2):
                    t0 = g * J + 2 * q
                    sp.wait_ge(pre_done, 2 * (BLOCKS + g) + q + 1)
                    if t0 + 2 < WIN:
                        sp.dma_start(rows(out[t0 * P:(t0 + 2) * P, :]), pre[q][:, :, :]).then_inc(out_done[q], 16)
                    else:
                        sp.dma_start(out[t0 * P:(t0 + 1) * P, :], pre[q][:, 0, :]).then_inc(out_done[q], 16)
                        sp.dma_start(out[(t0 + 1) * P:NODES, :], pre[q][0:TAILN, 1, :]).then_inc(out_done[q], 16)
                if g + 2 < GROUPS:
                    x_again(g + 2)
            sp.wait_ge(out_done[0], 16 * GROUPS)
            sp.wait_ge(out_done[1], 16 * (GROUPS + 1))

        @block.gpsimd
        def _(pool):
            nc.gpsimd.iota(part_id[:, :], [[0, 1]], base=0, channel_multiplier=1,
                           allow_small_or_imprecise_dtypes=True).then_inc(iota_done, 1)
            nc.gpsimd.iota(node_id[:, 0:P], [[1, P]], base=0, channel_multiplier=0,
                           allow_small_or_imprecise_dtypes=True).then_inc(iota_done, 1)
            nc.gpsimd.iota(node_id[:, P:WIN * P], [[1, (WIN - 1) * P]], base=P, channel_multiplier=0,
                           allow_small_or_imprecise_dtypes=True).then_inc(iota_wide, 1)

            def gather(b, rnd, par, wait=True):
                if wait:
                    pool.wait_ge(pre_done, 2 * b - 2)
                nc.gpsimd.tensor_copy(idx_now[par][:, :], src_col[:, bass.ds(b, 1), :].rearrange(
                    "p b j -> p (b j)")).then_inc(idx_copied, 1)
                copied = b + 1 if type(b) is int else pool.snap(b + 1)
                pool.wait_ge(idx_copied, copied)
                pool.sem_inc(idx_ready, 1)
                for j in range(J):
                    pool.indirect_dma_start(
                        out=hg[par][:, j, :], out_offset=None, in_=htab,
                        in_offset=bass.IndirectOffsetOnAxis(ap=idx_now[par][:, j:j + 1], axis=0),
                    ).then_inc(gathered[par], 16)

            pool.wait_ge(small_in, 80)
            for g in range(POOL_GROUPS):
                pool.wait_ge(acc_relu, g + 1)
                nc.gpsimd.tensor_tensor(
                    h_sb[:, g * J:(g + 1) * J, :], acc[:, g * J:(g + 1) * J, :],
                    b2["e"][:, :].rearrange("p (o f) -> p o f", o=1).to_broadcast([P, J, F]),
                    ALU.add).then_inc(h_pool, 1)
            pool.wait_ge(src_cols, 2)
            pool.wait_ge(wlo_done, 2)
            pool.wait_ge(htab_out, 16 * GROUPS)
            gather(0, 0, 0, wait=False)
            gather(1, 0, 1, wait=False)
            with pool.Fori(0, (BLOCKS - 2) // 2) as i:
                for par in range(2):
                    gather(2 * i + 2 + par, i + 1, par)

        @block.tensor
        def _(pe):
            pe.wait_ge(ident_done, 1)

            def index_T(tab, banks, ready, done):
                pe.wait_ge(ready, 1)
                for c in range(2):
                    for j in range(J):
                        last = nc.tensor.transpose(
                            banks[c][:, j * P:(j + 1) * P], tab[:, c, j * P:(j + 1) * P], ident[:, :])
                    last.then_inc(done, 1)

            def T(g):
                for k in range(KF):
                    if g > 0:
                        pe.wait_ge(nlo_done, 2 * g + k - 1)
                    for j in range(J):
                        last = nc.tensor.transpose(psT[k][:, j * P:(j + 1) * P],
                                                   acc[:, g * J + j, k * P:(k + 1) * P], ident[:, :])
                    last.then_inc(t_done, 1)

            def M1(b, par, kind, first=False):
                hi, lo = w1[kind]
                if kind == "e":
                    pe.wait_ge(elo_done, b + 1)
                else:
                    pe.wait_ge(nlo_done, 2 * (b - BLOCKS) + 2)
                for m in range(KH):
                    if m == 3:
                        pe.wait_ge(hfull_done, 4 * b + 1)
                    elif not first:
                        pe.wait_ge(hfull_done, 4 * b if m == 0 else 4 * b - 3 + m)
                    ps = psH[H_BANK[m]][:, :]
                    c = slice(m * P, (m + 1) * P)
                    for k in range(KF):
                        nc.tensor.matmul(ps, hi[:, k, c], eT_hi[par][:, k, :], start=(k == 0), stop=False)
                        nc.tensor.matmul(ps, hi[:, k, c], eT_lo[par][:, k, :], start=False, stop=False)
                        last = nc.tensor.matmul(ps, lo[:, k, c], eT_hi[par][:, k, :],
                                                start=False, stop=(k == KF - 1))
                    last.then_inc(m1_done, 1)

            def M2(b, par, kind, first=False):
                hi, lo = w2[kind]
                pe.wait_ge(hlo_done, 4 * b + 4)
                for j in range(J):
                    if j % 2 == 0 and not first:
                        pe.wait_ge(pre_done, 2 * b - 1 + j // 2)
                    ps = psM[j // 2][:, j % 2, :]
                    c = slice(j * P, (j + 1) * P)
                    for k in range(KH):
                        nc.tensor.matmul(ps, hid_hi[par][:, k, c], hi[:, k, :], start=(k == 0), stop=False)
                        nc.tensor.matmul(ps, hid_hi[par][:, k, c], lo[:, k, :], start=False, stop=False)
                        last = nc.tensor.matmul(ps, hid_lo[par][:, k, c], hi[:, k, :],
                                                start=False, stop=(k == KH - 1))
                    last.then_inc(m2_done, 1)

            extra = pe.alloc_register("pe_further_windows")
            pe.reg_mov(extra, 0)

            def sum_window(par, s):
                for j in range(J):
                    nc.tensor.matmul(psA[:, 0:F], s[:, j, :], msg_hi[par][:, j, :], start=(j == 0), stop=False)
                    last = nc.tensor.matmul(psA[:, 0:F], s[:, j, :], msg_lo[par][:, j, :],
                                            start=False, stop=(j == J - 1))
                return last

            def AGG(b, par, first=False):
                more = pe.value_load(win_row[0:1, bass.ds(4 * b + 1, 1)], min_val=0, max_val=WIN - 1)
                before = pe.snap(extra, min_val=0, max_val=BLOCKS * WIN)
                pe.wait_ge(mlo_done, 2 * b + 2)
                pe.wait_ge(sel_done, b + 1)
                if not first:
                    pe.wait_ge(added, b)
                    pe.wait_ge(addedx, before + 1)
                sum_window(par, sel[par]).then_inc(agg_done, 1)
                return before, more

            def AGGX(b, par, state):
                before, more = state
                with pe.If(more > 0):
                    with pe.Fori(1, more + 1) as w:
                        pe.wait_ge(added, b + 1)
                        pe.wait_ge(selx_done, before + w)
                        pe.wait_ge(addedx, before + w)
                        sum_window(par, sel_x).then_inc(aggx_done, 1)
                pe.reg_add(extra, extra, more)

            index_T(src_f, [psA[:, :], psH[2][:, :]], src_float, src_T)
            pe.wait_ge(src_cols, 2)
            pe.wait_ge(wlo_done, 1)
            M1(0, 0, "e", first=True)
            index_T(dst_f, [psM[q][:, :, :].rearrange("p a b -> p (a b)") for q in range(2)],
                    dst_float, dst_T)
            M1(1, 1, "e")
            pe.wait_ge(wlo_done, 2)
            pe.wait_ge(dst_cols, 2)
            M2(0, 0, "e", first=True)
            pe.wait_ge(wrow_in, 32)
            M1(2, 0, "e")
            state = AGG(0, 0, first=True)
            M2(1, 1, "e")
            AGGX(0, 0, state)
            with pe.Fori(0, (BLOCKS - 4) // 2) as i:
                for u in range(2):
                    b = 2 * i + 3 + u
                    M1(b, 1 - u, "e")
                    state = AGG(b - 2, 1 - u)
                    M2(b - 1, u, "e")
                    AGGX(b - 2, 1 - u, state)
            for b in range(BLOCKS - 1, BLOCKS + 2):
                if b < BLOCKS:
                    M1(b, b % 2, "e")
                state = AGG(b - 2, b % 2)
                if b - 1 < BLOCKS:
                    M2(b - 1, (b - 1) % 2, "e")
                AGGX(b - 2, b % 2, state)
            n_all = pe.snap(extra, min_val=0, max_val=BLOCKS * WIN)
            pe.wait_ge(added, BLOCKS)
            pe.wait_ge(addedx, n_all + 1)
            pe.wait_ge(wlo_done, 4)
            T(0)
            for g in range(GROUPS + 1):
                b = BLOCKS + g
                if g + 1 < GROUPS:
                    T(g + 1)
                if g < GROUPS:
                    M1(b, b % 2, "n")
                if g > 0:
                    M2(b - 1, (b - 1) % 2, "n")

        @block.scalar
        def _(act):
            for q in range(P // Q):
                act.dma_start(staged(hg[0], KF)[q * Q:(q + 1) * Q, :, :],
                              We1[2 * Q * q:2 * Q * (q + 1), :].rearrange("(k r) h -> r k h", r=Q)
                              ).then_inc(W1_IN, 16)
            act.dma_start(staged(hg[1], KH),
                          We2.rearrange("(k p) h -> p k h", p=P)).then_inc(W2_IN, 16)
            with nc.allow_non_contiguous_dma(reason="512 biases, once"):
                act.dma_start(b1["e"][:, :], be1.rearrange("(m p) -> p m", p=P)).then_inc(small_in, 16)
                act.dma_start(b1["n"][:, :], bn1.rearrange("(m p) -> p m", p=P)).then_inc(small_in, 16)
            for k, b in (("e", be2), ("n", bn2)):
                act.dma_start(b2[k][:, :], b.rearrange("(o f) -> o f", o=1).to_broadcast([P, F])
                              ).then_inc(small_in, 16)
            act.dma_start(eps_t[:, :], eps.rearrange("(o f) -> o f", o=1).to_broadcast([P, 1])
                          ).then_inc(small_in, 16)

            def w_hi(w_sem, loads, stage, k, dest):
                act.wait_ge(w_sem, 16 * loads)
                nc.scalar.copy(dest[:, :, :], staged(stage, k)).then_inc(whi_done, 1)

            def E_HI(b, par, first=False):
                act.wait_ge(tr_done, b + 1)
                if not first:
                    act.wait_ge(m1_done, 4 * b - 4)
                nc.scalar.copy(eT_hi[par][:, :, :], eT[:, :, :]).then_inc(ehi_done, 1)

            def NODE_HI(g):
                for k in range(KF):
                    act.wait_ge(t_done, 2 * g + k + 1)
                    act.wait_ge(m1_done, 4 * (BLOCKS + g) - 4)
                    nc.scalar.copy(eT_hi[g % 2][:, k, :], psT[k][:, :]).then_inc(nhi_done, 1)

            def HIDDEN(b, par, kind, first=0):
                if not first:
                    act.wait_ge(m2_done, 4 * b - 4)
                for m in range(KH):
                    act.wait_ge(m1_done, 4 * b + m + 1)
                    nc.scalar.activation(hid_hi[par][:, m, :], psH[H_BANK[m]][:, :], ACT.Relu,
                                         bias=b1[kind][:, m:m + 1])
                    if first < 2 or m >= 2:
                        act.wait_ge(hlo_done, 4 * b + m - 1)
                    nc.scalar.activation(hid[:, m % 2, :], psH[H_BANK[m]][:, :], ACT.Relu,
                                         bias=b1[kind][:, m:m + 1]).then_inc(hfull_done, 1)

            def MSG_HI(b, par):
                for q in range(2):
                    act.wait_ge(pre_done, 2 * b + q + 1)
                    nc.scalar.activation(msg_hi[par][:, 2 * q:2 * q + 2, :], pre[q][:, :, :], ACT.Relu
                                         ).then_inc(mhi_done, 1)

            w_hi(W1_IN, P // Q, hg[0], KF, w1["e"][0])
            E_HI(0, 0, first=True)
            w_hi(W2_IN, 1, hg[1], KH, w2["e"][0])
            act.wait_ge(ln_var, 1)
            nc.scalar.activation(std0[:, :], var_e[:, :], ACT.Sqrt).then_inc(ln_sqrt, 1)
            for g in range(GROUPS):
                act.wait_ge(ln_z, g + 1)
                nc.scalar.activation(acc[:, g * J:(g + 1) * J, :], h_sb[:, g * J:(g + 1) * J, :], ACT.Relu
                                     ).then_inc(acc_relu, 1)
            act.wait_ge(small_in, 80)
            HIDDEN(0, 0, "e", first=2)
            E_HI(1, 1, first=True)
            act.wait_ge(eps_done, 1)
            for g in range(GROUPS):
                if g < POOL_GROUPS:
                    act.wait_ge(h_pool, g + 1)
                else:
                    act.wait_ge(h_dve, g - POOL_GROUPS + 1)
                nc.scalar.activation(acc[:, g * J:(g + 1) * J, :], acc[:, g * J:(g + 1) * J, :], ACT.Copy,
                                     scale=ep1[:, 0:1]).then_inc(acc_init, 1)
            HIDDEN(1, 1, "e", first=1)
            E_HI(2, 0)
            MSG_HI(0, 0)
            with act.Fori(0, LOOP) as i:
                for u in range(2):
                    b = 2 * i + 2 + u
                    HIDDEN(b, u, "e")
                    E_HI(b + 1, 1 - u)
                    MSG_HI(b - 1, 1 - u)
            b = BLOCKS - 2
            HIDDEN(b, 0, "e")
            E_HI(b + 1, 1)
            MSG_HI(b - 1, 1)
            act.wait_ge(tr_done, BLOCKS)
            act.dma_start(staged(e_in[0], KF), Wn1.rearrange("(k p) h -> p k h", p=P)).then_inc(WN1_IN, 16)
            act.dma_start(staged(e_in[1], KH), Wn2.rearrange("(k p) h -> p k h", p=P)).then_inc(WN2_IN, 16)
            HIDDEN(b + 1, 1, "e")
            MSG_HI(b, 0)
            w_hi(WN1_IN, 1, e_in[0], KF, w1["n"][0])
            w_hi(WN2_IN, 1, e_in[1], KH, w2["n"][0])
            MSG_HI(b + 1, 1)
            NODE_HI(0)
            for g in range(GROUPS):
                if g + 1 < GROUPS:
                    NODE_HI(g + 1)
                HIDDEN(BLOCKS + g, g % 2, "n")

        @block.vector
        def _(dve):
            step = [0]

            def chain(ins):
                step[0] += 1
                ins.then_inc(prep, 1)
                dve.wait_ge(prep, step[0])

            nc.vector.memset(src_i[:, 1, :], 0).then_inc(pads_done, 1)
            nc.vector.memset(dst_i[:, 1, :], -1).then_inc(pads_done, 1)
            nc.vector.memset(acc[:, WIN - 1, :], 0.0).then_inc(pads_done, 1)
            dve.wait_ge(iota_done, 2)
            nc.vector.tensor_scalar(ident[:, :], node_id[:, 0:P], part_id[:, 0:1], None, ALU.is_equal
                                    ).then_inc(ident_done, 1)

            def index_float(to, table):
                return nc.vector.tensor_copy(to.rearrange("b c (g s) -> b c g s", s=Q),
                                             table.rearrange("b c (s g) -> b c g s", s=Q))

            def index_cols(banks, col, ready, done):
                for c in range(2):
                    many = min(P, BLOCKS - c * P)
                    dve.wait_ge(ready, c + 1)
                    nc.vector.tensor_copy(col[:, c * P:c * P + many, :],
                                          banks[c].rearrange("p (j b) -> p b j", j=J)[:, 0:many, :]
                                          ).then_inc(done, 1)

            def w_lo(n, stage, k, hi, lo):
                dve.wait_ge(whi_done, n + 1)
                nc.vector.tensor_tensor(lo[:, :, :], staged(stage, k), hi[:, :, :].bitcast(F32), ALU.subtract
                                        ).then_inc(wlo_done, 1)

            def TR(b, rnd, par):
                dve.wait_ge(e_loaded[par], (P // Q) * 16 * (rnd + 1))
                if type(b) is not int or b > 0:
                    dve.wait_ge(elo_done, b)
                nc.vector.transpose(eT[:, :, :].rearrange("p k (g s) -> p g k s", s=Q),
                                    e_in[par][:, :, :].rearrange("p g (k r) -> p g k r", r=Q)
                                    ).then_inc(tr_done, 1)

            def E_LO(b, par, first=False):
                dve.wait_ge(ehi_done, b + 1)
                if not first:
                    dve.wait_ge(m1_done, 4 * b - 4)
                nc.vector.tensor_tensor(eT_lo[par][:, :, :], eT[:, :, :], eT_hi[par][:, :, :].bitcast(F32),
                                        ALU.subtract).then_inc(elo_done, 1)

            def NODE_LO(g):
                for k in range(KF):
                    dve.wait_ge(nhi_done, 2 * g + k + 1)
                    dve.wait_ge(m1_done, 4 * (BLOCKS + g) - 4)
                    nc.vector.tensor_tensor(eT_lo[g % 2][:, k, :], psT[k][:, :],
                                            eT_hi[g % 2][:, k, :].bitcast(F32), ALU.subtract
                                            ).then_inc(nlo_done, 1)

            def HID_LO(b, par, first=False):
                for m in range(KH):
                    dve.wait_ge(hfull_done, 4 * b + m + 1)
                    if m == 0 and not first:
                        dve.wait_ge(m2_done, 4 * b - 4)
                    nc.vector.tensor_tensor(hid_lo[par][:, m, :], hid[:, m % 2, :],
                                            hid_hi[par][:, m, :].bitcast(F32), ALU.subtract).then_inc(hlo_done, 1)

            def MSG(b, rnd, par):
                for q in range(2):
                    dve.wait_ge(m2_done, 4 * b + 2 * q + 2)
                    if q == 0:
                        dve.wait_ge(gathered[par], 16 * J * rnd + 16 * J)
                    nc.vector.tensor_tensor(pre[q][:, :, :], psM[q][:, :, :], hg[par][:, 2 * q:2 * q + 2, :],
                                            ALU.add).then_inc(pre_done, 1)
                for q in range(2):
                    dve.wait_ge(mhi_done, 2 * b + q + 1)
                    nc.vector.scalar_tensor_tensor(msg_lo[par][:, 2 * q:2 * q + 2, :], pre[q][:, :, :], 0.0,
                                                   msg_hi[par][:, 2 * q:2 * q + 2, :].bitcast(F32),
                                                   ALU.max, ALU.subtract).then_inc(mlo_done, 1)

            extra = dve.alloc_register("dve_further_windows")
            dve.reg_mov(extra, 0)

            def select(dest, col, b, start):
                return nc.vector.tensor_tensor(
                    dest[:, :, :],
                    node_id[:, bass.ds(start, P)].rearrange("p (o c) -> p o c", o=1).to_broadcast([P, J, P]),
                    col[:, bass.ds(b, 1), :].rearrange("p o j -> p j o").to_broadcast([P, J, P]),
                    ALU.is_equal)

            def add_window(w):
                a = acc[:, bass.ds(w, 1), :].rearrange("p o f -> p (o f)")
                return nc.vector.tensor_tensor(a, psA[:, 0:F], a, ALU.add)

            def windows(b):
                w_first = dve.value_load(win_row[0:1, bass.ds(4 * b, 1)], min_val=0, max_val=WIN - 1)
                more = dve.value_load(win_row[0:1, bass.ds(4 * b + 1, 1)], min_val=0, max_val=WIN - 1)
                two = dve.value_load(win_row[0:1, bass.ds(4 * b + 2, 1)], min_val=0, max_val=1)
                return w_first, more, two

            further = dve.alloc_register("dve_further_window")

            def window_at(w_first, k):
                dve.reg_add(further, w_first, k)
                return dve.snap(further, min_val=0, max_val=WIN - 1)

            def SEL(b, par, first=False):
                more = dve.value_load(win_row[0:1, bass.ds(4 * b + 1, 1)], min_val=0, max_val=WIN - 1)
                with dve.If(more > 0):
                    w_first = dve.value_load(win_row[0:1, bass.ds(4 * b, 1)], min_val=0, max_val=WIN - 1)
                    if not first:
                        dve.wait_ge(agg_done, b - 1)
                    select(sel[par], dst_col, b, w_first * P).then_inc(sel_done, 1)
                with dve.Else():
                    if not first:
                        dve.wait_ge(agg_done, b - 1)
                    select(sel[par], mod_col, b, 0).then_inc(sel_done, 1)

            def ADD(b, w):
                w_first, _, two = w
                with dve.If(two > 0):
                    both = ((w_first, in_first), (window_at(w_first, 1), in_next))
                    dve.wait_ge(agg_done, b + 1)
                    for w, mask in both:
                        a = acc[:, bass.ds(w, 1), :].rearrange("p o f -> p (o f)")
                        last = nc.vector.scalar_tensor_tensor(a, psA[:, 0:F], mask[:, bass.ds(b, 1)], a,
                                                              ALU.mult, ALU.add)
                    last.then_inc(added, 1)
                with dve.Else():
                    dve.wait_ge(agg_done, b + 1)
                    add_window(w_first).then_inc(added, 1)

            def ADDX(b, w):
                w_first, more, _ = w
                with dve.If(more > 0):
                    before = dve.snap(extra, min_val=0, max_val=BLOCKS * WIN)
                    select(sel_x, dst_col, b, window_at(w_first, 1) * P).then_inc(selx_done, 1)
                    with dve.Fori(1, more + 1) as k:
                        dve.wait_ge(aggx_done, before + k)
                        add_window(window_at(w_first, k)).then_inc(addedx, 1)
                        with dve.If(more > k):
                            select(sel_x, dst_col, b, window_at(w_first, k + 1) * P).then_inc(selx_done, 1)
                dve.reg_add(extra, extra, more)

            dve.wait_ge(src_in, 48)
            index_float(src_f, src_i).then_inc(src_float, 1)
            TR(0, 0, 0)
            w_lo(0, hg[0], KF, *w1["e"])
            index_cols([psA[:, :], psH[2][:, :]], src_col, src_T, src_cols)
            E_LO(0, 0, first=True)
            for g in range(GROUPS):
                dve.wait_ge(x_in[g], 32 if g == GROUPS - 1 else 16)
                for t in range(g * J, (g + 1) * J):
                    last = nc.vector.bn_stats(stats[:, t, :], acc[:, t, :])
            chain(last)
            for t in range(WIN):
                last = nc.vector.bn_aggr(mv[:, t, :], stats[:, t, :])
            chain(last)
            nc.vector.tensor_scalar(var_e[:, :], mv[:, :, 1], LN_EPS, None, ALU.add).then_inc(ln_var, 1)
            w_lo(1, hg[1], KH, *w2["e"])
            dve.wait_ge(ln_sqrt, 1)
            chain(nc.vector.reciprocal(std1[:, :], std0[:, :]))
            chain(nc.vector.tensor_tensor(std1[:, :], std1[:, :], var_e[:, :], ALU.mult))
            chain(nc.vector.tensor_tensor(std1[:, :], std1[:, :], std0[:, :], ALU.add))
            chain(nc.vector.tensor_scalar(std2[:, :], std1[:, :], 0.5, None, ALU.mult))
            chain(nc.vector.reciprocal(rstd[:, :], std2[:, :]))
            dve.wait_ge(src_T, 2)
            for g in range(GROUPS):
                for t in range(g * J, (g + 1) * J):
                    last = nc.vector.tensor_scalar(h_sb[:, t, :], acc[:, t, :], mv[:, t, 0:1], rstd[:, t:t + 1],
                                                   ALU.subtract, ALU.mult)
                last.then_inc(ln_z, 1)
            dve.wait_ge(small_in, 80)
            nc.vector.tensor_scalar(ep1[:, :], eps_t[:, :], 1.0, None, ALU.add).then_inc(eps_done, 1)
            dve.wait_ge(dst_in, 48)
            index_float(dst_f, dst_i).then_inc(dst_float, 1)
            for g in range(POOL_GROUPS, GROUPS):
                dve.wait_ge(acc_relu, g + 1)
                nc.vector.tensor_tensor(
                    h_sb[:, g * J:(g + 1) * J, :], acc[:, g * J:(g + 1) * J, :],
                    b2["e"][:, :].rearrange("p (o f) -> p o f", o=1).to_broadcast([P, J, F]),
                    ALU.add).then_inc(h_dve, 1)
            TR(1, 0, 1)
            HID_LO(0, 0, first=True)
            E_LO(1, 1, first=True)
            index_cols([psM[q][:, :, :].rearrange("p a b -> p (a b)") for q in range(2)],
                       dst_col, dst_T, dst_cols)
            dve.wait_ge(dst_float, 1)
            chain(nc.vector.tensor_scalar(dst_i[:, :, :], dst_i[:, :, :], FAR - 1, None, ALU.bitwise_and))
            nc.vector.tensor_reduce(lim_f[:, :, 0:1], dst_i[:, :, :], AX.X, ALU.min)
            chain(nc.vector.tensor_reduce(lim_f[:, :, 1:2], dst_f[:, :, :], AX.X, ALU.max))
            chain(nc.vector.tensor_copy(lim_i[:, :, :], lim_f[:, :, :]))
            nc.vector.tensor_scalar(win_i[:, :, :], lim_i[:, :, :], 7, None, ALU.arith_shift_right)
            chain(nc.vector.tensor_tensor(wide[:, :, 0:1], lim_f[:, :, 1:2], lim_f[:, :, 0:1], ALU.subtract))
            chain(nc.vector.tensor_scalar(wide[:, :, 1:2], wide[:, :, 0:1], float(P), None, ALU.is_ge))
            nc.vector.tensor_copy(win_t[:, :, 0:1], win_i[:, :, 0:1]).then_inc(win_done, 1)
            nc.vector.scalar_tensor_tensor(lo_mod[:, :], win_i[:, :, 0], -float(P), lim_f[:, :, 0],
                                           ALU.mult, ALU.add).then_inc(win_done, 1)
            chain(nc.vector.tensor_tensor(wide[:, :, 0:1], win_i[:, :, 1:2], win_i[:, :, 0:1], ALU.subtract))
            chain(nc.vector.tensor_tensor(wide[:, :, 1:2], wide[:, :, 0:1], wide[:, :, 1:2], ALU.mult))
            nc.vector.tensor_copy(win_t[:, :, 1:2], wide[:, :, 1:2])
            nc.vector.memset(win_t[:, :, 3:4], 0).then_inc(win_done, 1)
            nc.vector.tensor_tensor(win_t[:, :, 2:3], wide[:, :, 0:1], wide[:, :, 1:2], ALU.subtract
                                    ).then_inc(win_done, 1)
            TR(2, 1, 0)
            HID_LO(1, 1, first=True)
            E_LO(2, 0)
            dst_ci = dst_i[:, :, :].rearrange("p c e -> p (c e)")[:, 0:BLOCKS * J]
            col = dst_col[:, :, :].rearrange("p b j -> p (b j)")
            mod = mod_col[:, :, :].rearrange("p b j -> p (b j)")
            dve.wait_ge(dst_cols, 2)
            chain(nc.vector.tensor_copy(dst_ci, col))
            chain(nc.vector.tensor_scalar(dst_ci, dst_ci, 7, None, ALU.arith_shift_right))
            chain(nc.vector.scalar_tensor_tensor(mod, dst_ci, -float(P), col, ALU.mult, ALU.add))
            over = dst_f[:, 0, 0:J]
            chain(nc.vector.tensor_scalar(over, dst_col[:, BLOCKS - 1, :], 0.0, float(FAR), ALU.is_lt, ALU.mult))
            chain(nc.vector.tensor_tensor(mod_col[:, BLOCKS - 1, :], mod_col[:, BLOCKS - 1, :], over, ALU.add))
            MSG(0, 0, 0)
            nc.vector.memset(mark[:, :], 0.0).then_inc(addedx, 1)
            dve.wait_ge(iota_wide, 1)
            dve.wait_ge(wrow_in, 32)
            dve.wait_ge(acc_init, GROUPS)
            nc.vector.tensor_scalar(in_first[:, :], lo_row[:, :], part_id[:, 0:1], None, ALU.is_le)
            chain(nc.vector.tensor_scalar(in_next[:, :], lo_row[:, :], part_id[:, 0:1], None, ALU.is_gt))

            def iteration(b, half, u, first=False):
                if type(b) is not int or b + 1 < BLOCKS:
                    TR(b + 1, half + u, 1 - u)
                w = windows(b - 2)
                if type(b) is not int or b < BLOCKS:
                    HID_LO(b, u)
                ADD(b - 2, w)
                if type(b) is not int or b + 1 < BLOCKS:
                    E_LO(b + 1, 1 - u)
                if type(b) is not int or b - 1 < BLOCKS:
                    SEL(b - 1, 1 - u, first=first)
                    MSG(b - 1, half - 1 + u, 1 - u)
                ADDX(b - 2, w)

            SEL(0, 0, first=True)
            iteration(2, 1, 0, first=True)
            iteration(3, 1, 1)
            with dve.Fori(0, LOOP - 1) as i:
                for u in range(2):
                    iteration(2 * i + 4 + u, i + 2, u)
            for b in range(BLOCKS - 2, BLOCKS + 2):
                iteration(b, b // 2, b % 2)
                if b == BLOCKS:
                    w_lo(2, e_in[0], KF, *w1["n"])
                    w_lo(3, e_in[1], KH, *w2["n"])
            NODE_LO(0)
            for g in range(GROUPS + 1):
                b = BLOCKS + g
                if g + 1 < GROUPS:
                    NODE_LO(g + 1)
                if g < GROUPS:
                    dve.wait_ge(x_back[g % 2], 16 * (g // 2 + 1 + (g == GROUPS - 1)))
                    xb = hg[g % 2][:, :, :]
                    nc.vector.tensor_tensor(
                        xb, xb, b2["n"][:, :].rearrange("p (o f) -> p o f", o=1).to_broadcast([P, J, F]),
                        ALU.add).then_inc(xb_done, 1)
                    HID_LO(b, b % 2)
                if g > 0:
                    dve.wait_ge(xb_done, g)
                    for q in range(2):
                        dve.wait_ge(m2_done, 4 * (b - 1) + 2 * q + 2)
                        if g > 1:
                            dve.wait_ge(out_done[q], 16 * (g - 1))
                        nc.vector.tensor_tensor(pre[q][:, :, :], psM[q][:, :, :],
                                                hg[(g - 1) % 2][:, 2 * q:2 * q + 2, :], ALU.add
                                                ).then_inc(pre_done, 1)


_INS = ["x", "src", "dst", "edge_attr_256", "L0_gnn_We1", "L0_gnn_be1", "L0_gnn_We2", "L0_gnn_be2",
        "L0_gnn_Wn1", "L0_gnn_bn1", "L0_gnn_Wn2", "L0_gnn_bn2", "L0_gnn_eps"]


def kernel(**inputs):
    import numpy as _np
    import concourse.bacc as _bacc
    from concourse import mybir as _mybir
    from concourse.bass_utils import run_bass_kernel_spmd as _run

    nc = _bacc.Bacc("TRN2", target_bir_lowering=False, num_devices=1)
    arrays, args = {}, []
    for name in _INS:
        a = _np.ascontiguousarray(inputs[name])
        arrays[f"in_{name}_dram"] = a
        args.append(nc.dram_tensor(f"in_{name}_dram", a.shape, _mybir.dt.from_np(a.dtype), kind="ExternalInput").ap())
    args.append(nc.dram_tensor("out_0_dram", (NODES, F), _mybir.dt.float32, kind="ExternalOutput").ap())
    gnn_program(nc, *args)
    r = _run(nc, [arrays], core_ids=[0])
    return r.results[0]["out_0_dram"]
```

```python
from contextlib import ExitStack

import concourse.bass as bass
from concourse import mybir

ALU = mybir.AluOpType
ACT = mybir.ActivationFunctionType
AX = mybir.AxisListType
F32 = mybir.dt.float32
F32R = mybir.dt.float32r
I32 = mybir.dt.int32

P = 128
NODES = 2500
EDGES = 82500
F = 256
HID = 512
EB = 512
J = EB // P
Q = 32
S = EB // Q
KF = F // P
KH = HID // P
BLOCKS = -(-EDGES // EB)
LEFT = EDGES - (BLOCKS - 1) * EB
JL = -(-LEFT // P)
SL = JL * P // Q
SKIP = (JL * P - LEFT) // SL
WIN = -(-NODES // P)
TAILN = NODES - (WIN - 1) * P
GROUPS = WIN // J
DVE_GROUPS = 2
LOOP = (BLOCKS - 4) // 2
LN_EPS = 1e-5
FAR = 8192


def gnn_program(nc, x, src, dst, edge, We1, be1, We2, be2, Wn1, bn1, Wn2, bn2, eps, out):
    assert SKIP * SL == JL * P - LEFT and WIN % J == 0 and BLOCKS % 2 == 0 and JL <= 2 and BLOCKS > P and EB == 4 * P
    ctx = ExitStack()
    with ctx:
        def sb(name, shape, dt=F32):
            return ctx.enter_context(nc.sbuf_tensor(name, shape, dt))

        def bank(name, shape):
            return ctx.enter_context(nc.psum_tensor(name, shape, F32))

        def sem(name):
            return ctx.enter_context(nc.semaphore(name))

        htab = nc.dram_tensor("h_rows", (WIN * P, F), F32, kind="Internal").ap()
        wtab = nc.dram_tensor("windows", (2 * P, 4), I32, kind="Internal").ap()
        ltab = nc.dram_tensor("smallest", (2 * P,), I32, kind="Internal").ap()

        h_sb = sb("h_sb", [P, WIN, F])
        acc = sb("acc", [P, WIN, F])
        w1 = {k: [sb(f"w1{k}_{p}", [P, KF, HID], F32R) for p in ("hi", "lo")] for k in ("e", "n")}
        w2 = {k: [sb(f"w2{k}_{p}", [P, KH, F], F32R) for p in ("hi", "lo")] for k in ("e", "n")}
        b1 = {k: sb(f"b1{k}", [P, KH]) for k in ("e", "n")}
        b2 = {k: sb(f"b2{k}", [P, F]) for k in ("e", "n")}
        ep1 = sb("ep1", [P, 1])
        e_in = [sb(f"e_in{i}", [P, S, 2 * Q]) for i in range(2)]
        eT = sb("eT", [P, KF, EB])
        eT_hi = [sb(f"eT_hi{i}", [P, KF, EB], F32R) for i in range(2)]
        eT_lo = [sb(f"eT_lo{i}", [P, KF, EB], F32R) for i in range(2)]
        hid = sb("hid", [P, 2, EB])
        hid_hi = [sb(f"hid_hi{i}", [P, KH, EB], F32R) for i in range(2)]
        hid_lo = [sb(f"hid_lo{i}", [P, KH, EB], F32R) for i in range(2)]
        hg = [sb(f"hg{i}", [P, J, F]) for i in range(2)]
        pre = [sb(f"pre{q}", [P, 2, F]) for q in range(2)]
        msg_hi = [sb(f"msg_hi{i}", [P, J, F], F32R) for i in range(2)]
        msg_lo = [sb(f"msg_lo{i}", [P, J, F], F32R) for i in range(2)]
        sel = [sb(f"sel{i}", [P, J, P], F32R) for i in range(2)]
        sel_x = sb("sel_x", [P, J, P], F32R)
        node_id = sb("node_id", [P, WIN * P])
        part_id = sb("part_id", [P, 1])
        ident = sb("ident", [P, P])
        dst_i = sb("dst_i", [P, 2, EB], I32)
        dst_f = sb("dst_f", [P, 2, EB])
        src_i, src_f = (
            h_sb[:, 4 * n:4 * n + 4, :].rearrange("p t f -> p (t f)").rearrange("p (c e) -> p c e", c=2)
            for n in range(2))
        src_i = src_i.bitcast(I32)
        lim_f = sb("lim_f", [P, 2, 2])
        lim_i = sb("lim_i", [P, 2, 2], I32)
        win_i = sb("win_i", [P, 2, 2], I32)
        wide = sb("wide", [P, 2, 2])
        win_t = sb("win_t", [P, 2, 4], I32)
        lo_mod = sb("lo_mod", [P, 2], I32)
        win_row = sb("win_row", [1, 4 * BLOCKS], I32)
        lo_row = sb("lo_row", [P, BLOCKS], I32)
        in_first = sb("in_first", [P, BLOCKS])
        in_next = sb("in_next", [P, BLOCKS])
        dst_col = sb("dst_col", [P, BLOCKS, J])
        mod_col = sb("mod_col", [P, BLOCKS, J])
        src_col = sb("src_col", [P, BLOCKS, J], I32)
        idx_now = [sb(f"idx_now{i}", [P, J], I32) for i in range(2)]
        stats = sb("stats", [P, WIN, 6])
        mv = sb("mv", [P, WIN, 2])
        var_e = sb("var_e", [P, WIN])
        std0 = sb("std0", [P, WIN])
        std1 = sb("std1", [P, WIN])
        std2 = sb("std2", [P, WIN])
        rstd = sb("rstd", [P, WIN])
        eps_t = sb("eps_t", [P, 1])
        warm = sb("warm", [P, 1])
        mark = sb("mark", [1, 1])

        psT = [bank(f"psT{k}", [P, EB]) for k in range(KF)]
        psH = [bank(f"psH{i}", [P, EB]) for i in range(3)]
        psM = [bank(f"psM{q}", [P, 2, F]) for q in range(2)]
        psA = bank("psA", [P, EB])
        H_BANK = [0, 1, 2, 0]
        src_banks = [psM[q][:, :, :].rearrange("p a b -> p (a b)") for q in range(2)]
        dst_banks = [psT[k][:, :] for k in range(KF)]

        x_in = [sem(f"x_in{g}") for g in range(GROUPS)]
        src_in = sem("src_in")
        dst_in = sem("dst_in")
        w_in = [sem(f"w_in{i}") for i in range(4)]
        small_in = sem("small_in")
        e_loaded = [sem(f"e_loaded{i}") for i in range(2)]
        gathered = [sem(f"gathered{i}") for i in range(2)]
        htab_out = sem("htab_out")
        wtab_out = sem("wtab_out")
        wrow_in = sem("wrow_in")
        out_done = [sem(f"out_done{i}") for i in range(2)]
        iota_done = sem("iota_done")
        iota_wide = sem("iota_wide")
        prep = sem("prep")
        pads_done = sem("pads_done")
        ident_done = sem("ident_done")
        src_float = sem("src_float")
        dst_float = sem("dst_float")
        src_T = sem("src_T")
        dst_T = sem("dst_T")
        src_cols = sem("src_cols")
        dst_cols = sem("dst_cols")
        win_done = sem("win_done")
        ln_var = sem("ln_var")
        ln_sqrt = sem("ln_sqrt")
        rstd_done = sem("rstd_done")
        z_done = sem("z_done")
        h_pool = sem("h_pool")
        h_dve = sem("h_dve")
        relu_act = sem("relu_act")
        acc_init = sem("acc_init")
        eps_done = sem("eps_done")
        whi_done = sem("whi_done")
        wlo_done = sem("wlo_done")
        tr_done = sem("tr_done")
        ehi_done = sem("ehi_done")
        elo_done = sem("elo_done")
        t_done = sem("t_done")
        nhi_done = sem("nhi_done")
        nlo_done = sem("nlo_done")
        m1_done = sem("m1_done")
        hfull_done = sem("hfull_done")
        hlo_done = sem("hlo_done")
        m2_done = sem("m2_done")
        pre_done = sem("pre_done")
        mhi_done = sem("mhi_done")
        mlo_done = sem("mlo_done")
        sel_done = sem("sel_done")
        agg_done = sem("agg_done")
        added = sem("added")
        selx_done = sem("selx_done")
        aggx_done = sem("aggx_done")
        addedx = sem("addedx")
        idx_copied = sem("idx_copied")
        idx_ready = sem("idx_ready")
        x_back = [sem(f"x_back{i}") for i in range(2)]
        xb_done = sem("xb_done")

        block = ctx.enter_context(nc.Block())

        def staged(t, k):
            return t[:, :, :].rearrange("p a b -> p (a b)").rearrange("p (k h) -> p k h", k=k)

        def rows(t):
            return t.rearrange("(t p) f -> p t f", p=P)

        W1_IN, W2_IN, WN1_IN, WN2_IN = w_in
        FULLN = (WIN - 1) * P

        @block.sync
        def _(sp):
            sp.wait_ge(pads_done, 3)
            last = BLOCKS - 1 - P

            def last_row(table):
                return table[last:last + 1, 1, :].rearrange("o (s e) -> o s e", e=S)[:, :, 0:SL]

            sp.dma_start(dst_i[:, 0, :], dst[0:P * EB].rearrange("(s e) -> s e", e=EB)).then_inc(dst_in, 16)
            sp.dma_start(dst_i[0:last, 1, :],
                         dst[P * EB:(BLOCKS - 1) * EB].rearrange("(s e) -> s e", e=EB)).then_inc(dst_in, 16)
            sp.dma_start(last_row(dst_i)[:, SKIP:Q, :],
                         dst[EDGES - LEFT:EDGES].rearrange("(o s e) -> o s e", o=1, e=SL)).then_inc(dst_in, 16)

            def load(par, start, per=S):
                for q in range(P // Q):
                    sp.dma_start(e_in[par][q * Q:(q + 1) * Q, 0:per, :],
                                 edge[bass.ds(start, per * Q), 2 * Q * q:2 * Q * (q + 1)].rearrange(
                                     "(s g) f -> s g f", g=per)).then_inc(e_loaded[par], 16)

            load(0, 0)
            sp.dma_start(src_i[:, 0, :], src[0:P * EB].rearrange("(s e) -> s e", e=EB)).then_inc(src_in, 16)
            sp.dma_start(src_i[0:last, 1, :],
                         src[P * EB:(BLOCKS - 1) * EB].rearrange("(s e) -> s e", e=EB)).then_inc(src_in, 16)
            sp.dma_start(last_row(src_i),
                         src[EDGES - JL * P:EDGES].rearrange("(o s e) -> o s e", o=1, e=SL)).then_inc(src_in, 16)
            for g in range(GROUPS):
                full = min((g + 1) * EB, FULLN)
                sp.dma_start(acc[:, g * J:full // P, :], rows(x[g * EB:full, :])).then_inc(x_in[g], 16)
                if g == 1:
                    sp.dma_start(staged(hg[1], KH),
                                  We2.rearrange("(k p) h -> p k h", p=P)).then_inc(W2_IN, 16)
            sp.dma_start(acc[0:TAILN, WIN - 1, :], x[FULLN:NODES, :]).then_inc(x_in[GROUPS - 1], 16)
            load(1, EB)
            sp.wait_ge(win_done, 4)
            sp.dma_start(wtab.rearrange("(c p) w -> p c w", p=P), win_t[:, :, :]).then_inc(wtab_out, 16)
            with nc.allow_non_contiguous_dma(reason="256 numbers, once"):
                sp.dma_start(ltab.rearrange("(c p) -> p c", p=P), lo_mod[:, :]).then_inc(wtab_out, 16)
            sp.wait_ge(wtab_out, 32)
            sp.dma_start(win_row[:, :], wtab[0:BLOCKS, :].rearrange("(o b) w -> o (b w)", o=1)
                         ).then_inc(wrow_in, 16)
            sp.dma_start(lo_row[:, :], ltab[0:BLOCKS].rearrange("(o b) -> o b", o=1).to_broadcast([P, BLOCKS])
                         ).then_inc(wrow_in, 16)
            sp.wait_ge(tr_done, 1)
            load(0, 2 * EB)
            sp.wait_ge(tr_done, 2)
            load(1, 3 * EB)
            for g in [2, 3, 0, 1, 4]:
                if g < DVE_GROUPS:
                    sp.wait_ge(h_dve, g + 1)
                else:
                    sp.wait_ge(h_pool, g - DVE_GROUPS + 1)
                sp.dma_start(rows(htab[g * EB:(g + 1) * EB, :]), h_sb[:, g * J:(g + 1) * J, :]
                             ).then_inc(htab_out, 16)
            with sp.Fori(0, LOOP - 1) as i:
                for par in range(2):
                    sp.wait_ge(tr_done, 2 * i + par + 3)
                    load(par, (2 * i + par + 4) * EB)
            sp.wait_ge(tr_done, BLOCKS - 3)
            load(0, (BLOCKS - 2) * EB)
            sp.wait_ge(tr_done, BLOCKS - 2)
            load(1, EDGES - JL * P, SL)

            def x_again(g):
                if g < 2:
                    sp.wait_ge(pre_done, 2 * (BLOCKS - 2 + g) + 2)
                if (g + 1) * J < WIN:
                    sp.dma_start(hg[g % 2][:, :, :], rows(x[g * EB:(g + 1) * EB, :])).then_inc(x_back[g % 2], 16)
                else:
                    sp.dma_start(hg[g % 2][:, 0:J - 1, :], rows(x[g * EB:FULLN, :])).then_inc(x_back[g % 2], 16)
                    sp.dma_start(hg[g % 2][0:TAILN, J - 1, :], x[FULLN:NODES, :]).then_inc(x_back[g % 2], 16)

            x_again(0)
            x_again(1)
            for g in range(GROUPS):
                for q in range(2):
                    t0 = g * J + 2 * q
                    sp.wait_ge(pre_done, 2 * (BLOCKS + g) + q + 1)
                    if t0 + 2 < WIN:
                        sp.dma_start(rows(out[t0 * P:(t0 + 2) * P, :]), pre[q][:, :, :]).then_inc(out_done[q], 16)
                    else:
                        sp.dma_start(out[t0 * P:(t0 + 1) * P, :], pre[q][:, 0, :]).then_inc(out_done[q], 16)
                        sp.dma_start(out[(t0 + 1) * P:NODES, :], pre[q][0:TAILN, 1, :]).then_inc(out_done[q], 16)
                if g + 2 < GROUPS:
                    x_again(g + 2)
            sp.wait_ge(out_done[0], 16 * GROUPS)
            sp.wait_ge(out_done[1], 16 * (GROUPS + 1))

        @block.gpsimd
        def _(pool):
            nc.gpsimd.iota(part_id[:, :], [[0, 1]], base=0, channel_multiplier=1,
                           allow_small_or_imprecise_dtypes=True).then_inc(iota_done, 1)
            nc.gpsimd.iota(node_id[:, 0:P], [[1, P]], base=0, channel_multiplier=0,
                           allow_small_or_imprecise_dtypes=True).then_inc(iota_done, 1)
            nc.gpsimd.iota(node_id[:, P:WIN * P], [[1, (WIN - 1) * P]], base=P, channel_multiplier=0,
                           allow_small_or_imprecise_dtypes=True).then_inc(iota_wide, 1)

            def gather(b, half, par, wait=True):
                if wait:
                    pool.wait_ge(pre_done, 2 * b - 2)
                nc.gpsimd.tensor_copy(idx_now[par][:, :], src_col[:, bass.ds(b, 1), :].rearrange(
                    "p b j -> p (b j)")).then_inc(idx_copied, 1)
                copied = b + 1 if type(b) is int else pool.snap(b + 1)
                pool.wait_ge(idx_copied, copied)
                pool.sem_inc(idx_ready, 1)
                for j in range(J):
                    pool.indirect_dma_start(
                        out=hg[par][:, j, :], out_offset=None, in_=htab,
                        in_offset=bass.IndirectOffsetOnAxis(ap=idx_now[par][:, j:j + 1], axis=0),
                    ).then_inc(gathered[par], 16)

            def w_lo(n, stage, k, hi, lo):
                pool.wait_ge(whi_done, n + 1)
                nc.gpsimd.tensor_tensor(lo[:, :, :], staged(stage, k), hi[:, :, :].bitcast(F32), ALU.subtract
                                        ).then_inc(wlo_done, 1)

            w_lo(0, hg[0], KF, *w1["e"])
            w_lo(1, hg[1], KH, *w2["e"])
            for m in range(KH):
                pool.wait_ge(hfull_done, m + 1)
                nc.gpsimd.tensor_tensor(hid_lo[0][:, m, :], hid[:, m % 2, :],
                                        hid_hi[0][:, m, :].bitcast(F32), ALU.subtract).then_inc(hlo_done, 1)
            pool.wait_ge(small_in, 80)
            for g in range(DVE_GROUPS, GROUPS):
                pool.wait_ge(relu_act, g - DVE_GROUPS + 1)
                nc.gpsimd.tensor_tensor(
                    h_sb[:, g * J:(g + 1) * J, :], acc[:, g * J:(g + 1) * J, :],
                    b2["e"][:, :].rearrange("p (o f) -> p o f", o=1).to_broadcast([P, J, F]),
                    ALU.add).then_inc(h_pool, 1)
            pool.wait_ge(src_cols, 2)
            pool.wait_ge(wlo_done, 2)
            pool.wait_ge(htab_out, 16 * GROUPS)
            gather(0, 0, 0, wait=False)
            gather(1, 0, 1, wait=False)
            with pool.Fori(0, (BLOCKS - 2) // 2) as i:
                for par in range(2):
                    gather(2 * i + 2 + par, i + 1, par)

        @block.tensor
        def _(pe):
            pe.wait_ge(ident_done, 1)

            def index_T(tab, banks, ready, done):
                pe.wait_ge(ready, 1)
                for c in range(2):
                    for j in range(J):
                        last = nc.tensor.transpose(
                            banks[c][:, j * P:(j + 1) * P], tab[:, c, j * P:(j + 1) * P], ident[:, :])
                    last.then_inc(done, 1)

            def T(g):
                for k in range(KF):
                    if g > 0:
                        pe.wait_ge(nlo_done, 2 * g + k - 1)
                    for j in range(J):
                        last = nc.tensor.transpose(psT[k][:, j * P:(j + 1) * P],
                                                   acc[:, g * J + j, k * P:(k + 1) * P], ident[:, :])
                    last.then_inc(t_done, 1)

            def M1(b, par, kind, first=False, sets=J):
                hi, lo = w1[kind]
                n = sets * P
                if kind == "e":
                    pe.wait_ge(elo_done, b + 1)
                else:
                    pe.wait_ge(nlo_done, 2 * (b - BLOCKS) + 2)
                for m in range(KH):
                    if m == 3:
                        pe.wait_ge(hfull_done, 4 * b + 1)
                    elif not first:
                        pe.wait_ge(hfull_done, 4 * b if m == 0 else 4 * b - 3 + m)
                    ps = psH[H_BANK[m]][:, 0:n]
                    c = slice(m * P, (m + 1) * P)
                    for k in range(KF):
                        nc.tensor.matmul(ps, hi[:, k, c], eT_hi[par][:, k, 0:n], start=(k == 0), stop=False)
                        nc.tensor.matmul(ps, hi[:, k, c], eT_lo[par][:, k, 0:n], start=False, stop=False)
                        last = nc.tensor.matmul(ps, lo[:, k, c], eT_hi[par][:, k, 0:n],
                                                start=False, stop=(k == KF - 1))
                    last.then_inc(m1_done, 1)

            def M2(b, par, kind, first=False, sets=J):
                hi, lo = w2[kind]
                pe.wait_ge(hlo_done, 4 * b + 4)
                for j in range(sets):
                    if j % 2 == 0 and not first:
                        pe.wait_ge(pre_done, 2 * b - 1 + j // 2)
                    ps = psM[j // 2][:, j % 2, :]
                    c = slice(j * P, (j + 1) * P)
                    for k in range(KH):
                        nc.tensor.matmul(ps, hid_hi[par][:, k, c], hi[:, k, :], start=(k == 0), stop=False)
                        nc.tensor.matmul(ps, hid_hi[par][:, k, c], lo[:, k, :], start=False, stop=False)
                        last = nc.tensor.matmul(ps, hid_lo[par][:, k, c], hi[:, k, :],
                                                start=False, stop=(k == KH - 1))
                    last.then_inc(m2_done, 1 if j + 1 < sets else 1 + J - sets)

            extra = pe.alloc_register("pe_further_windows")
            pe.reg_mov(extra, 0)

            def sum_window(par, s, sets):
                for j in range(sets):
                    nc.tensor.matmul(psA[:, 0:F], s[:, j, :], msg_hi[par][:, j, :], start=(j == 0), stop=False)
                    last = nc.tensor.matmul(psA[:, 0:F], s[:, j, :], msg_lo[par][:, j, :],
                                            start=False, stop=(j == sets - 1))
                return last

            def AGG(b, par, first=False, sets=J):
                more = pe.value_load(win_row[0:1, bass.ds(4 * b + 1, 1)], min_val=0, max_val=WIN - 1)
                before = pe.snap(extra, min_val=0, max_val=BLOCKS * WIN)
                pe.wait_ge(mlo_done, 2 * b + 2)
                pe.wait_ge(sel_done, b + 1)
                if not first:
                    pe.wait_ge(added, b)
                    pe.wait_ge(addedx, before + 1)
                sum_window(par, sel[par], sets).then_inc(agg_done, 1)
                return before, more

            def AGGX(b, par, state, sets=J):
                before, more = state
                with pe.If(more > 0):
                    with pe.Fori(1, more + 1) as w:
                        pe.wait_ge(added, b + 1)
                        pe.wait_ge(selx_done, before + w)
                        pe.wait_ge(addedx, before + w)
                        sum_window(par, sel_x, sets).then_inc(aggx_done, 1)
                pe.reg_add(extra, extra, more)

            index_T(dst_f, dst_banks, dst_float, dst_T)
            index_T(src_f, src_banks, src_float, src_T)
            pe.wait_ge(wlo_done, 1)
            M1(0, 0, "e", first=True)
            M1(1, 1, "e")
            pe.wait_ge(wlo_done, 2)
            pe.wait_ge(src_cols, 2)
            M2(0, 0, "e", first=True)
            M1(2, 0, "e")
            M2(1, 1, "e")
            pe.wait_ge(wrow_in, 32)
            state = AGG(0, 0, first=True)
            AGGX(0, 0, state)
            with pe.Fori(0, LOOP) as i:
                for u in range(2):
                    b = 2 * i + 3 + u
                    M1(b, 1 - u, "e")
                    state = AGG(b - 2, 1 - u)
                    M2(b - 1, u, "e")
                    AGGX(b - 2, 1 - u, state)
            b = BLOCKS - 1
            M1(b, 1, "e", sets=JL)
            state = AGG(b - 2, 1)
            M2(b - 1, 0, "e")
            AGGX(b - 2, 1, state)
            M2(b, 1, "e", sets=JL)
            for par, sets in ((0, J), (1, JL)):
                state = AGG(b - 1 + par, par, sets=sets)
                AGGX(b - 1 + par, par, state, sets)
            n_all = pe.snap(extra, min_val=0, max_val=BLOCKS * WIN)
            pe.wait_ge(added, BLOCKS)
            pe.wait_ge(addedx, n_all + 1)
            T(0)
            pe.wait_ge(wlo_done, 3)
            for g in range(GROUPS + 1):
                b = BLOCKS + g
                if g + 1 < GROUPS:
                    T(g + 1)
                if g < GROUPS:
                    M1(b, b % 2, "n")
                if g > 0:
                    if g == 1:
                        pe.wait_ge(wlo_done, 4)
                    M2(b - 1, (b - 1) % 2, "n")

        @block.scalar
        def _(act):
            for q in range(P // Q):
                act.dma_start(staged(hg[0], KF)[q * Q:(q + 1) * Q, :, :],
                              We1[2 * Q * q:2 * Q * (q + 1), :].rearrange("(k r) h -> r k h", r=Q)
                              ).then_inc(W1_IN, 16)
            with nc.allow_non_contiguous_dma(reason="512 biases, once"):
                act.dma_start(b1["e"][:, :], be1.rearrange("(m p) -> p m", p=P)).then_inc(small_in, 16)
                act.dma_start(b1["n"][:, :], bn1.rearrange("(m p) -> p m", p=P)).then_inc(small_in, 16)
            for k, b in (("e", be2), ("n", bn2)):
                act.dma_start(b2[k][:, :], b.rearrange("(o f) -> o f", o=1).to_broadcast([P, F])
                              ).then_inc(small_in, 16)
            act.dma_start(eps_t[:, :], eps.rearrange("(o f) -> o f", o=1).to_broadcast([P, 1])
                          ).then_inc(small_in, 16)


            def w_hi(w_sem, loads, stage, k, dest):
                act.wait_ge(w_sem, 16 * loads)
                nc.scalar.copy(dest[:, :, :], staged(stage, k)).then_inc(whi_done, 1)

            def E_HI(b, par, first=False):
                act.wait_ge(tr_done, b + 1)
                if not first:
                    act.wait_ge(m1_done, 4 * b - 4)
                nc.scalar.copy(eT_hi[par][:, :, :], eT[:, :, :]).then_inc(ehi_done, 1)

            def NODE_HI(g):
                for k in range(KF):
                    act.wait_ge(t_done, 2 * g + k + 1)
                    act.wait_ge(m1_done, 4 * (BLOCKS + g) - 4)
                    nc.scalar.copy(eT_hi[g % 2][:, k, :], psT[k][:, :]).then_inc(nhi_done, 1)

            def HIDDEN(b, par, kind, first=0, chunks=range(KH), sets=J):
                if not first:
                    act.wait_ge(m2_done, 4 * b - 4)
                for m in chunks:
                    act.wait_ge(m1_done, 4 * b + m + 1)
                    n = sets * P
                    nc.scalar.activation(hid_hi[par][:, m, 0:n], psH[H_BANK[m]][:, 0:n], ACT.Relu,
                                         bias=b1[kind][:, m:m + 1])
                    if first < 2 or m >= 2:
                        act.wait_ge(hlo_done, 4 * b + m - 1)
                    nc.scalar.activation(hid[:, m % 2, 0:n], psH[H_BANK[m]][:, 0:n], ACT.Relu,
                                         bias=b1[kind][:, m:m + 1]).then_inc(hfull_done, 1)

            def MSG_HI(b, par):
                for q in range(2):
                    act.wait_ge(pre_done, 2 * b + q + 1)
                    nc.scalar.activation(msg_hi[par][:, 2 * q:2 * q + 2, :], pre[q][:, :, :], ACT.Relu
                                         ).then_inc(mhi_done, 1)

            def RELU(g):
                if g < DVE_GROUPS:
                    act.wait_ge(h_dve, g + 1)
                else:
                    act.wait_ge(z_done, g - DVE_GROUPS + 1)
                a = acc[:, g * J:(g + 1) * J, :]
                nc.scalar.activation(a, a, ACT.Relu).then_inc(relu_act, 1)

            def ACC_INIT(g):
                act.wait_ge(relu_act, GROUPS)
                if g >= DVE_GROUPS:
                    act.wait_ge(h_pool, g - DVE_GROUPS + 1)
                a = acc[:, g * J:(g + 1) * J, :]
                nc.scalar.activation(a, a, ACT.Copy, scale=ep1[:, 0:1]).then_inc(acc_init, 1)

            def index_cols(banks, col, ready, done):
                for c in range(2):
                    many = min(P, BLOCKS - c * P)
                    act.wait_ge(ready, c + 1)
                    nc.scalar.copy(col[:, c * P:c * P + many, :],
                                   banks[c].rearrange("p (j b) -> p b j", j=J)[:, 0:many, :]
                                   ).then_inc(done, 1)

            act.wait_ge(iota_done, 1)
            nc.scalar.activation(warm[:, :], part_id[:, :], ACT.Sqrt)
            w_hi(W1_IN, P // Q, hg[0], KF, w1["e"][0])
            E_HI(0, 0, first=True)
            index_cols(dst_banks, dst_col, dst_T, dst_cols)
            index_cols(src_banks, src_col, src_T, src_cols)
            w_hi(W2_IN, 1, hg[1], KH, w2["e"][0])
            act.wait_ge(small_in, 80)
            HIDDEN(0, 0, "e", first=2, chunks=(0, 1, 2))
            act.wait_ge(ln_var, 1)
            nc.scalar.activation(std0[:, :], var_e[:, :], ACT.Sqrt).then_inc(ln_sqrt, 1)
            HIDDEN(0, 0, "e", first=2, chunks=(3,))
            E_HI(1, 1, first=True)
            for g in range(DVE_GROUPS, GROUPS):
                RELU(g)
            HIDDEN(1, 1, "e", first=1, chunks=(0, 1))
            for g in range(DVE_GROUPS):
                RELU(g)
            HIDDEN(1, 1, "e", first=1, chunks=(2, 3))
            E_HI(2, 0)
            act.wait_ge(eps_done, 1)
            for g in range(3):
                ACC_INIT(g)
            HIDDEN(2, 0, "e")
            MSG_HI(0, 0)
            E_HI(3, 1)
            for g in range(3, GROUPS):
                ACC_INIT(g)
            MSG_HI(1, 1)
            with act.Fori(0, LOOP) as i:
                for u in range(2):
                    b = 2 * i + 3 + u
                    HIDDEN(b, 1 - u, "e")
                    E_HI(b + 1, u)
                    MSG_HI(b - 1, u)
            b = BLOCKS - 2
            act.wait_ge(tr_done, BLOCKS)
            act.dma_start(staged(e_in[0], KF), Wn1.rearrange("(k p) h -> p k h", p=P)).then_inc(WN1_IN, 16)
            act.dma_start(staged(e_in[1], KH), Wn2.rearrange("(k p) h -> p k h", p=P)).then_inc(WN2_IN, 16)
            HIDDEN(b + 1, 1, "e", sets=JL)
            w_hi(WN1_IN, 1, e_in[0], KF, w1["n"][0])
            w_hi(WN2_IN, 1, e_in[1], KH, w2["n"][0])
            MSG_HI(b, 0)
            act.wait_ge(pre_done, 2 * BLOCKS)
            nc.scalar.activation(msg_hi[1][:, 0:JL, :], pre[0][:, 0:JL, :], ACT.Relu).then_inc(mhi_done, 2)
            NODE_HI(0)
            for g in range(GROUPS):
                if g + 1 < GROUPS:
                    NODE_HI(g + 1)
                HIDDEN(BLOCKS + g, g % 2, "n")

        @block.vector
        def _(dve):
            step = [0]

            def chain(ins):
                step[0] += 1
                ins.then_inc(prep, 1)
                dve.wait_ge(prep, step[0])

            nc.vector.memset(src_i[:, 1, :], 0).then_inc(pads_done, 1)
            nc.vector.memset(dst_i[:, 1, :], -1).then_inc(pads_done, 1)
            nc.vector.memset(acc[:, WIN - 1, :], 0.0).then_inc(pads_done, 1)
            dve.wait_ge(iota_done, 2)
            nc.vector.tensor_scalar(ident[:, :], node_id[:, 0:P], part_id[:, 0:1], None, ALU.is_equal
                                    ).then_inc(ident_done, 1)

            def index_float(to, table):
                return nc.vector.tensor_copy(to.rearrange("b c (g s) -> b c g s", s=Q),
                                             table.rearrange("b c (s g) -> b c g s", s=Q))

            def w_lo(n, stage, k, hi, lo):
                dve.wait_ge(whi_done, n + 1)
                nc.vector.tensor_tensor(lo[:, :, :], staged(stage, k), hi[:, :, :].bitcast(F32), ALU.subtract
                                        ).then_inc(wlo_done, 1)

            def TR(b, half, par):
                dve.wait_ge(e_loaded[par], (P // Q) * 16 * (half + 1))
                if type(b) is not int or b > 0:
                    dve.wait_ge(elo_done, b)
                nc.vector.transpose(eT[:, :, :].rearrange("p k (g s) -> p g k s", s=Q),
                                    e_in[par][:, :, :].rearrange("p g (k r) -> p g k r", r=Q)
                                    ).then_inc(tr_done, 1)

            def E_LO(b, par, first=False):
                dve.wait_ge(ehi_done, b + 1)
                if not first:
                    dve.wait_ge(m1_done, 4 * b - 4)
                nc.vector.tensor_tensor(eT_lo[par][:, :, :], eT[:, :, :], eT_hi[par][:, :, :].bitcast(F32),
                                        ALU.subtract).then_inc(elo_done, 1)

            def NODE_LO(g):
                for k in range(KF):
                    dve.wait_ge(nhi_done, 2 * g + k + 1)
                    dve.wait_ge(m1_done, 4 * (BLOCKS + g) - 4)
                    nc.vector.tensor_tensor(eT_lo[g % 2][:, k, :], psT[k][:, :],
                                            eT_hi[g % 2][:, k, :].bitcast(F32), ALU.subtract
                                            ).then_inc(nlo_done, 1)

            def HID_LO(b, par, first=False, chunks=range(KH), sets=J):
                for m in chunks:
                    dve.wait_ge(hfull_done, 4 * b + m + 1)
                    if m == 0 and not first:
                        dve.wait_ge(m2_done, 4 * b - 4)
                    n = sets * P
                    nc.vector.tensor_tensor(hid_lo[par][:, m, 0:n], hid[:, m % 2, 0:n],
                                            hid_hi[par][:, m, 0:n].bitcast(F32), ALU.subtract).then_inc(hlo_done, 1)

            def MSG(b, half, par):
                for q in range(2):
                    dve.wait_ge(m2_done, 4 * b + 2 * q + 2)
                    if q == 0:
                        dve.wait_ge(gathered[par], 16 * J * half + 16 * J)
                    nc.vector.tensor_tensor(pre[q][:, :, :], psM[q][:, :, :], hg[par][:, 2 * q:2 * q + 2, :],
                                            ALU.add).then_inc(pre_done, 1)
                for q in range(2):
                    dve.wait_ge(mhi_done, 2 * b + q + 1)
                    nc.vector.scalar_tensor_tensor(msg_lo[par][:, 2 * q:2 * q + 2, :], pre[q][:, :, :], 0.0,
                                                   msg_hi[par][:, 2 * q:2 * q + 2, :].bitcast(F32),
                                                   ALU.max, ALU.subtract).then_inc(mlo_done, 1)

            extra = dve.alloc_register("dve_further_windows")
            dve.reg_mov(extra, 0)

            def select(dest, col, b, start):
                return nc.vector.tensor_tensor(
                    dest[:, :, :],
                    node_id[:, bass.ds(start, P)].rearrange("p (o c) -> p o c", o=1).to_broadcast([P, J, P]),
                    col[:, bass.ds(b, 1), :].rearrange("p o j -> p j o").to_broadcast([P, J, P]),
                    ALU.is_equal)

            def add_window(w):
                a = acc[:, bass.ds(w, 1), :].rearrange("p o f -> p (o f)")
                return nc.vector.tensor_tensor(a, psA[:, 0:F], a, ALU.add)

            def windows(b):
                w_first = dve.value_load(win_row[0:1, bass.ds(4 * b, 1)], min_val=0, max_val=WIN - 1)
                more = dve.value_load(win_row[0:1, bass.ds(4 * b + 1, 1)], min_val=0, max_val=WIN - 1)
                two = dve.value_load(win_row[0:1, bass.ds(4 * b + 2, 1)], min_val=0, max_val=1)
                return w_first, more, two

            further = dve.alloc_register("dve_further_window")

            def window_at(w_first, k):
                dve.reg_add(further, w_first, k)
                return dve.snap(further, min_val=0, max_val=WIN - 1)

            def SEL(b, par, first=False):
                more = dve.value_load(win_row[0:1, bass.ds(4 * b + 1, 1)], min_val=0, max_val=WIN - 1)
                with dve.If(more > 0):
                    w_first = dve.value_load(win_row[0:1, bass.ds(4 * b, 1)], min_val=0, max_val=WIN - 1)
                    if not first:
                        dve.wait_ge(agg_done, b - 1)
                    select(sel[par], dst_col, b, w_first * P).then_inc(sel_done, 1)
                with dve.Else():
                    if not first:
                        dve.wait_ge(agg_done, b - 1)
                    select(sel[par], mod_col, b, 0).then_inc(sel_done, 1)

            def ADD(b, w):
                w_first, _, two = w
                with dve.If(two > 0):
                    both = ((w_first, in_first), (window_at(w_first, 1), in_next))
                    dve.wait_ge(agg_done, b + 1)
                    for w, mask in both:
                        a = acc[:, bass.ds(w, 1), :].rearrange("p o f -> p (o f)")
                        last = nc.vector.scalar_tensor_tensor(a, psA[:, 0:F], mask[:, bass.ds(b, 1)], a,
                                                              ALU.mult, ALU.add)
                    last.then_inc(added, 1)
                with dve.Else():
                    dve.wait_ge(agg_done, b + 1)
                    add_window(w_first).then_inc(added, 1)

            def ADDX(b, w):
                w_first, more, _ = w
                with dve.If(more > 0):
                    before = dve.snap(extra, min_val=0, max_val=BLOCKS * WIN)
                    select(sel_x, dst_col, b, window_at(w_first, 1) * P).then_inc(selx_done, 1)
                    with dve.Fori(1, more + 1) as k:
                        dve.wait_ge(aggx_done, before + k)
                        add_window(window_at(w_first, k)).then_inc(addedx, 1)
                        with dve.If(more > k):
                            select(sel_x, dst_col, b, window_at(w_first, k + 1) * P).then_inc(selx_done, 1)
                dve.reg_add(extra, extra, more)

            dve.wait_ge(dst_in, 48)
            index_float(dst_f, dst_i).then_inc(dst_float, 1)
            dve.wait_ge(dst_float, 1)
            chain(nc.vector.tensor_scalar(dst_i[:, :, :], dst_i[:, :, :], FAR - 1, None, ALU.bitwise_and))
            nc.vector.tensor_reduce(lim_f[:, :, 0:1], dst_i[:, :, :], AX.X, ALU.min)
            chain(nc.vector.tensor_reduce(lim_f[:, :, 1:2], dst_f[:, :, :], AX.X, ALU.max))
            chain(nc.vector.tensor_copy(lim_i[:, :, :], lim_f[:, :, :]))
            nc.vector.tensor_scalar(win_i[:, :, :], lim_i[:, :, :], 7, None, ALU.arith_shift_right)
            chain(nc.vector.tensor_tensor(wide[:, :, 0:1], lim_f[:, :, 1:2], lim_f[:, :, 0:1], ALU.subtract))
            chain(nc.vector.tensor_scalar(wide[:, :, 1:2], wide[:, :, 0:1], float(P), None, ALU.is_ge))
            nc.vector.tensor_copy(win_t[:, :, 0:1], win_i[:, :, 0:1]).then_inc(win_done, 1)
            nc.vector.scalar_tensor_tensor(lo_mod[:, :], win_i[:, :, 0], -float(P), lim_f[:, :, 0],
                                           ALU.mult, ALU.add).then_inc(win_done, 1)
            chain(nc.vector.tensor_tensor(wide[:, :, 0:1], win_i[:, :, 1:2], win_i[:, :, 0:1], ALU.subtract))
            chain(nc.vector.tensor_tensor(wide[:, :, 1:2], wide[:, :, 0:1], wide[:, :, 1:2], ALU.mult))
            nc.vector.tensor_copy(win_t[:, :, 1:2], wide[:, :, 1:2])
            nc.vector.memset(win_t[:, :, 3:4], 0).then_inc(win_done, 1)
            nc.vector.tensor_tensor(win_t[:, :, 2:3], wide[:, :, 0:1], wide[:, :, 1:2], ALU.subtract
                                    ).then_inc(win_done, 1)
            TR(0, 0, 0)
            dve.wait_ge(src_in, 48)
            index_float(src_f, src_i).then_inc(src_float, 1)
            for g in range(GROUPS):
                dve.wait_ge(x_in[g], 32 if g == GROUPS - 1 else 16)
                for t in range(g * J, (g + 1) * J):
                    last = nc.vector.bn_stats(stats[:, t, :], acc[:, t, :])
                if g == 0:
                    E_LO(0, 0, first=True)
            chain(last)
            for t in range(WIN):
                last = nc.vector.bn_aggr(mv[:, t, :], stats[:, t, :])
            chain(last)
            nc.vector.tensor_scalar(var_e[:, :], mv[:, :, 1], LN_EPS, None, ALU.add).then_inc(ln_var, 1)
            TR(1, 0, 1)
            dve.wait_ge(ln_sqrt, 1)
            chain(nc.vector.reciprocal(std1[:, :], std0[:, :]))
            chain(nc.vector.tensor_tensor(std1[:, :], std1[:, :], var_e[:, :], ALU.mult))
            chain(nc.vector.tensor_tensor(std1[:, :], std1[:, :], std0[:, :], ALU.add))
            chain(nc.vector.tensor_scalar(std2[:, :], std1[:, :], 0.5, None, ALU.mult))
            nc.vector.reciprocal(rstd[:, :], std2[:, :]).then_inc(rstd_done, 1)
            dve.wait_ge(small_in, 80)
            nc.vector.tensor_scalar(ep1[:, :], eps_t[:, :], 1.0, None, ALU.add).then_inc(eps_done, 1)
            dve.wait_ge(rstd_done, 1)
            dve.wait_ge(src_T, 2)
            for g in [*range(DVE_GROUPS, GROUPS), *range(DVE_GROUPS)]:
                for t in range(g * J, (g + 1) * J):
                    last = nc.vector.tensor_scalar(acc[:, t, :], acc[:, t, :], mv[:, t, 0:1], rstd[:, t:t + 1],
                                                   ALU.subtract, ALU.mult)
                last.then_inc(z_done, 1)
                if g == DVE_GROUPS:
                    E_LO(1, 1, first=True)
            for g in range(DVE_GROUPS):
                dve.wait_ge(z_done, GROUPS - DVE_GROUPS + g + 1)
                c = slice(g * J, (g + 1) * J)
                nc.vector.scalar_tensor_tensor(
                    h_sb[:, c, :], acc[:, c, :], 0.0,
                    b2["e"][:, :].rearrange("p (o f) -> p o f", o=1).to_broadcast([P, J, F]),
                    ALU.max, ALU.add).then_inc(h_dve, 1)
            dve.wait_ge(hlo_done, KH)
            HID_LO(1, 1, first=True, chunks=(0, 1))
            TR(2, 1, 0)
            HID_LO(1, 1, first=True, chunks=(2, 3))
            E_LO(2, 0)
            dst_ci = dst_i[:, :, :].rearrange("p c e -> p (c e)")[:, 0:BLOCKS * J]
            col = dst_col[:, :, :].rearrange("p b j -> p (b j)")
            mod = mod_col[:, :, :].rearrange("p b j -> p (b j)")
            dve.wait_ge(dst_cols, 2)
            chain(nc.vector.tensor_copy(dst_ci, col))
            chain(nc.vector.tensor_scalar(dst_ci, dst_ci, 7, None, ALU.arith_shift_right))
            chain(nc.vector.scalar_tensor_tensor(mod, dst_ci, -float(P), col, ALU.mult, ALU.add))
            over = dst_f[:, 0, 0:J]
            chain(nc.vector.tensor_scalar(over, dst_col[:, BLOCKS - 1, :], 0.0, float(FAR), ALU.is_lt, ALU.mult))
            chain(nc.vector.tensor_tensor(mod_col[:, BLOCKS - 1, :], mod_col[:, BLOCKS - 1, :], over, ALU.add))
            nc.vector.memset(mark[:, :], 0.0).then_inc(addedx, 1)
            dve.wait_ge(iota_wide, 1)
            dve.wait_ge(wrow_in, 32)
            nc.vector.tensor_scalar(in_first[:, :], lo_row[:, :], part_id[:, 0:1], None, ALU.is_le)
            chain(nc.vector.tensor_scalar(in_next[:, :], lo_row[:, :], part_id[:, 0:1], None, ALU.is_gt))

            def iteration(b, half, u):
                TR(b + 1, half + u, 1 - u)
                w = windows(b - 2)
                HID_LO(b, u)
                ADD(b - 2, w)
                E_LO(b + 1, 1 - u)
                SEL(b - 1, 1 - u)
                MSG(b - 1, half - 1 + u, 1 - u)
                ADDX(b - 2, w)

            TR(3, 1, 1)
            HID_LO(2, 0, chunks=(0, 1))
            MSG(0, 0, 0)
            HID_LO(2, 0, chunks=(2, 3))
            SEL(0, 0, first=True)
            w = windows(0)
            E_LO(3, 1)
            dve.wait_ge(acc_init, GROUPS)
            ADD(0, w)
            SEL(1, 1, first=True)
            MSG(1, 0, 1)
            ADDX(0, w)
            iteration(3, 1, 1)
            with dve.Fori(0, LOOP - 1) as i:
                for u in range(2):
                    iteration(2 * i + 4 + u, i + 2, u)
            b = BLOCKS - 1
            iteration(b - 1, b // 2, 0)
            w = windows(b - 2)
            HID_LO(b, 1, sets=JL)
            ADD(b - 2, w)
            SEL(b - 1, 0)
            SEL(b, 1)
            next_w = windows(b - 1)
            MSG(b - 1, b // 2, 0)
            ADDX(b - 2, w)
            dve.wait_ge(mlo_done, 2 * b)
            dve.wait_ge(m2_done, J * b + J)
            dve.wait_ge(gathered[1], 16 * J * (b // 2) + 16 * J)
            nc.vector.tensor_tensor(pre[0][:, 0:JL, :], psM[0][:, 0:JL, :], hg[1][:, 0:JL, :], ALU.add
                                    ).then_inc(pre_done, 2)
            dve.wait_ge(mhi_done, 2 * b + 2)
            nc.vector.scalar_tensor_tensor(msg_lo[1][:, 0:JL, :], pre[0][:, 0:JL, :], 0.0,
                                           msg_hi[1][:, 0:JL, :].bitcast(F32), ALU.max, ALU.subtract
                                           ).then_inc(mlo_done, 2)
            ADD(b - 1, next_w)
            ADDX(b - 1, next_w)
            w_lo(2, e_in[0], KF, *w1["n"])
            w = windows(b)
            ADD(b, w)
            ADDX(b, w)
            NODE_LO(0)
            w_lo(3, e_in[1], KH, *w2["n"])
            for g in range(GROUPS + 1):
                b = BLOCKS + g
                if g + 1 < GROUPS:
                    NODE_LO(g + 1)
                if g < GROUPS:
                    dve.wait_ge(x_back[g % 2], 16 * (g // 2 + 1 + (g == GROUPS - 1)))
                    xb = hg[g % 2][:, :, :]
                    nc.vector.tensor_tensor(
                        xb, xb, b2["n"][:, :].rearrange("p (o f) -> p o f", o=1).to_broadcast([P, J, F]),
                        ALU.add).then_inc(xb_done, 1)
                    HID_LO(b, b % 2)
                if g > 0:
                    dve.wait_ge(xb_done, g)
                    for q in range(2):
                        dve.wait_ge(m2_done, 4 * (b - 1) + 2 * q + 2)
                        if g > 1:
                            dve.wait_ge(out_done[q], 16 * (g - 1))
                        nc.vector.tensor_tensor(pre[q][:, :, :], psM[q][:, :, :],
                                                hg[(g - 1) % 2][:, 2 * q:2 * q + 2, :], ALU.add
                                                ).then_inc(pre_done, 1)


_INS = ["x", "src", "dst", "edge_attr_256", "L0_gnn_We1", "L0_gnn_be1", "L0_gnn_We2", "L0_gnn_be2",
        "L0_gnn_Wn1", "L0_gnn_bn1", "L0_gnn_Wn2", "L0_gnn_bn2", "L0_gnn_eps"]


def kernel(**inputs):
    import numpy as _np
    import concourse.bacc as _bacc
    from concourse import mybir as _mybir
    from concourse.bass_utils import run_bass_kernel_spmd as _run

    nc = _bacc.Bacc("TRN2", target_bir_lowering=False, num_devices=1)
    arrays, args = {}, []
    for name in _INS:
        a = _np.ascontiguousarray(inputs[name])
        arrays[f"in_{name}_dram"] = a
        args.append(nc.dram_tensor(f"in_{name}_dram", a.shape, _mybir.dt.from_np(a.dtype), kind="ExternalInput").ap())
    args.append(nc.dram_tensor("out_0_dram", (NODES, F), _mybir.dt.float32, kind="ExternalOutput").ap())
    gnn_program(nc, *args)
    r = _run(nc, [arrays], core_ids=[0])
    return r.results[0]["out_0_dram"]
```
